# Optimizing a Trainium2 kernel written in Bass

```python
import numpy as np
import jax
import jax.numpy as jnp

def _softmax(x, axis=-1):
    return jax.nn.softmax(x, axis=axis)

def _gelu(x):
    return jax.nn.gelu(x, approximate=True)

def _silu(x):
    return jax.nn.silu(x)

def _sigmoid(x):
    return jax.nn.sigmoid(x)

def _layernorm(x, axis=-1, eps=1e-05):
    m = jnp.mean(x, axis=axis, keepdims=True)
    v = jnp.var(x, axis=axis, keepdims=True)
    return (x - m) / jnp.sqrt(v + eps)

def _scatter_add(tgt, idx, src, axis=0):
    return tgt.at[idx].add(src)

def _segment_sum(src, seg, n):
    return jax.ops.segment_sum(src, seg, n)
kernel_name = 'mk_pixart_seq_d1_seqx_r4_8f379d'

def setup_inputs(seed: int=0):
    np.random.seed(seed)
    _w = jnp.asarray

    def _rec_inputs():
        import jax
        import jax.numpy as jnp
        _rk = jax.random.key(seed)
        x = -0.0003929 + 0.9999 * jax.random.normal(jax.random.fold_in(_rk, 1), (8, 512, 256), jnp.float32)
        _lenS = 512 - jax.random.randint(jax.random.fold_in(_rk, 7), (8,), 0, max(1, 512 // 4) + 1, jnp.int32)
        _lenS2 = 64 - jax.random.randint(jax.random.fold_in(_rk, 8), (8,), 0, max(1, 64 // 4) + 1, jnp.int32)
        cond_1024 = 0.00782532 + 1.00527 * jax.random.normal(jax.random.fold_in(_rk, 11), (8, 256), jnp.float32)
        _ctx_1024P = jax.random.normal(jax.random.fold_in(_rk, 12), (8, 16, 256), jnp.float32)
        _ctx_1024c = jax.random.dirichlet(jax.random.fold_in(_rk, 512), 0.3 * jnp.ones((16,), jnp.float32), (8, 64))
        _ctx_1024t = jnp.einsum('bsk,bkd->bsd', _ctx_1024c, _ctx_1024P)
        _ctx_1024t = _ctx_1024t * jax.lax.rsqrt(jnp.mean(jnp.square(_ctx_1024t)) + 1e-12) * 0.953939
        ctx_1024 = -0.000761806 + 0.999296 * (_ctx_1024t + 0.3 * jax.random.normal(jax.random.fold_in(_rk, 612), (8, 64, 256), jnp.float32))
        return (x, cond_1024, ctx_1024)
    x, cond_1024, ctx_1024 = _rec_inputs()

    def _L0_xcond_setup():
        import jax, jax.numpy as jnp
        import numpy as np
        H = 256
        RH = 2 * H
        E = 3
        B, T, P = (8, 512, 64)
        LN_EPS = 1e-05

        def _layer_norm(x, gamma, beta):
            mu = jnp.mean(x, axis=-1, keepdims=True)
            var = jnp.mean(jnp.square(x - mu), axis=-1, keepdims=True)
            return (x - mu) * jax.lax.rsqrt(var + LN_EPS) * gamma + beta
        key = jax.random.key(seed)
        ks = jax.random.split(key, 24)
        s = lambda fan_in: 1.0 / np.sqrt(fan_in)
        inp = {'mix_hidden_states': jax.random.normal(ks[0], (B, T, H), jnp.float32), 'global_anchor': jax.random.normal(ks[1], (B, H), jnp.float32), 'prototype_bank': jax.random.normal(ks[2], (B, P, H), jnp.float32), 'ln_gamma': jnp.ones((H,), jnp.float32), 'ln_beta': jnp.zeros((H,), jnp.float32), 'Wq': jax.random.normal(ks[3], (H, H), jnp.float32) * s(H), 'Wk': jax.random.normal(ks[4], (H, H), jnp.float32) * s(H), 'Wv': jax.random.normal(ks[5], (H, H), jnp.float32) * s(H), 'router_W': jax.random.normal(ks[6], (3 * H, E), jnp.float32) * s(3 * H), 'router_b': jnp.zeros((E,), jnp.float32), 'e_w1': jax.random.normal(ks[7], (E, 3 * H, RH), jnp.float32) * s(3 * H), 'e_b1': jnp.zeros((E, RH), jnp.float32), 'e_w2': jax.random.normal(ks[8], (E, RH, H), jnp.float32) * s(RH), 'e_b2': jnp.zeros((E, H), jnp.float32), 'gate_w1': jax.random.normal(ks[9], (3 * H, H), jnp.float32) * s(3 * H), 'gate_b1': jnp.zeros((H,), jnp.float32), 'gate_w2': jax.random.normal(ks[10], (H, H), jnp.float32) * s(H), 'gate_b2': jnp.zeros((H,), jnp.float32), 'out_w': jax.random.normal(ks[11], (H, H), jnp.float32) * s(H), 'out_b': jnp.zeros((H,), jnp.float32)}
        return inp
    _L0_xcond_all = _L0_xcond_setup()
    _L0_xcond_in = {k: v for k, v in _L0_xcond_all.items() if k in ('ln_gamma', 'ln_beta', 'Wq', 'Wk', 'Wv', 'router_W', 'router_b', 'e_w1', 'e_b1', 'e_w2', 'e_b2', 'gate_w1', 'gate_b1', 'gate_w2', 'gate_b2', 'out_w', 'out_b')}
    del _L0_xcond_all
    return {'x': x, 'cond_1024': cond_1024, 'ctx_1024': ctx_1024, 'L0_xcond_ln_gamma': _L0_xcond_in['ln_gamma'], 'L0_xcond_ln_beta': _L0_xcond_in['ln_beta'], 'L0_xcond_Wq': _L0_xcond_in['Wq'], 'L0_xcond_Wk': _L0_xcond_in['Wk'], 'L0_xcond_Wv': _L0_xcond_in['Wv'], 'L0_xcond_router_W': _L0_xcond_in['router_W'], 'L0_xcond_router_b': _L0_xcond_in['router_b'], 'L0_xcond_e_w1': _L0_xcond_in['e_w1'], 'L0_xcond_e_b1': _L0_xcond_in['e_b1'], 'L0_xcond_e_w2': _L0_xcond_in['e_w2'], 'L0_xcond_e_b2': _L0_xcond_in['e_b2'], 'L0_xcond_gate_w1': _L0_xcond_in['gate_w1'], 'L0_xcond_gate_b1': _L0_xcond_in['gate_b1'], 'L0_xcond_gate_w2': _L0_xcond_in['gate_w2'], 'L0_xcond_gate_b2': _L0_xcond_in['gate_b2'], 'L0_xcond_out_w': _L0_xcond_in['out_w'], 'L0_xcond_out_b': _L0_xcond_in['out_b']}

def reference(x, cond_1024, ctx_1024, L0_xcond_ln_gamma, L0_xcond_ln_beta, L0_xcond_Wq, L0_xcond_Wk, L0_xcond_Wv, L0_xcond_router_W, L0_xcond_router_b, L0_xcond_e_w1, L0_xcond_e_b1, L0_xcond_e_w2, L0_xcond_e_b2, L0_xcond_gate_w1, L0_xcond_gate_b1, L0_xcond_gate_w2, L0_xcond_gate_b2, L0_xcond_out_w, L0_xcond_out_b):
    import jax
    import jax.numpy as jnp

    def _L0_xcond_ref(mix_hidden_states, global_anchor, prototype_bank, ln_gamma, ln_beta, Wq, Wk, Wv, router_W, router_b, e_w1, e_b1, e_w2, e_b2, gate_w1, gate_b1, gate_w2, gate_b2, out_w, out_b):
        import jax, jax.numpy as jnp
        import numpy as np
        H = 256
        RH = 2 * H
        E = 3
        B, T, P = (8, 512, 64)
        LN_EPS = 1e-05

        def _layer_norm(x, gamma, beta):
            mu = jnp.mean(x, axis=-1, keepdims=True)
            var = jnp.mean(jnp.square(x - mu), axis=-1, keepdims=True)
            return (x - mu) * jax.lax.rsqrt(var + LN_EPS) * gamma + beta
        x = mix_hidden_states
        nx = _layer_norm(x, ln_gamma, ln_beta)
        q = nx @ Wq
        k = prototype_bank @ Wk
        v = prototype_bank @ Wv
        scores = jnp.einsum('bth,bph->btp', q, k) * H ** (-0.5)
        weights = jax.nn.softmax(scores, axis=-1)
        evidence = jnp.einsum('btp,bph->bth', weights, v)
        anchor = jnp.broadcast_to(global_anchor[:, None, :], nx.shape)
        combined = jnp.concatenate([nx, evidence, anchor], axis=-1)
        router_logits = combined @ router_W + router_b
        router_probs = jax.nn.softmax(router_logits, axis=-1)
        h = jax.nn.silu(jnp.einsum('btc,ecr->bter', combined, e_w1) + e_b1)
        expert_out = jnp.einsum('bter,erh->bteh', h, e_w2) + e_b2
        routed = jnp.sum(expert_out * router_probs[..., None], axis=-2)
        g = jax.nn.sigmoid(jax.nn.silu(combined @ gate_w1 + gate_b1) @ gate_w2 + gate_b2)
        refined_delta = g * (routed @ out_w + out_b)
        return x + refined_delta
    x = _L0_xcond_ref(x, cond_1024, ctx_1024, L0_xcond_ln_gamma, L0_xcond_ln_beta, L0_xcond_Wq, L0_xcond_Wk, L0_xcond_Wv, L0_xcond_router_W, L0_xcond_router_b, L0_xcond_e_w1, L0_xcond_e_b1, L0_xcond_e_w2, L0_xcond_e_b2, L0_xcond_gate_w1, L0_xcond_gate_b1, L0_xcond_gate_w2, L0_xcond_gate_b2, L0_xcond_out_w, L0_xcond_out_b)
    return x

_drawn_inputs = setup_inputs


def setup_inputs(seed=0):
    import zlib

    import numpy as np

    out = dict(_drawn_inputs(seed))
    spreads = {'L0_xcond_ln_gamma': (1.0, 0.2),
     'L0_xcond_ln_beta': (0.0, 0.622),
     'L0_xcond_router_b': (0.0, 0.8),
     'L0_xcond_e_b1': (0.0, 0.41),
     'L0_xcond_e_b2': (0.0, 0.1),
     'L0_xcond_gate_b1': (0.0, 0.8),
     'L0_xcond_gate_b2': (0.0, 0.8),
     'L0_xcond_out_b': (0.0, 0.1)}
    factors = {}
    for name, (base, spread) in spreads.items():
        noise = np.random.default_rng([zlib.crc32(name.encode()), seed]).standard_normal(out[name].shape)
        drawn = base * np.exp(spread * noise) if base else spread * noise
        out[name] = jnp.asarray(drawn.astype(out[name].dtype))
    for name, factor in factors.items():
        out[name] = (out[name] * factor).astype(out[name].dtype)
    return out
```

```python
from contextlib import ExitStack

import concourse.bass as bass
from concourse import mybir

F32 = mybir.dt.float32
F32R = mybir.dt.float32r
ALU = mybir.AluOpType
ACT = mybir.ActivationFunctionType
AX_X = mybir.AxisListType.X

PART = 128
LN_EPS = 1e-05
SPLIT_PASSES = ((0, 0), (0, 1), (1, 0))
HI, LO = 0, 1


def build(nc, x, cond, ctx, ln_gamma, ln_beta, Wq, Wk, Wv, router_W, router_b,
          e_w1, e_b1, e_w2, e_b2, gate_w1, gate_b1, gate_w2, gate_b2, out_w, out_b, out):
    B, T, H = x.shape
    NP = ctx.shape[1]
    E, _, R = e_w1.shape
    KC = H // PART
    NT = T // PART
    GB = H // PART
    EB = R // PART
    NB = GB + E * EB
    NCOL = NB * PART
    RP = 4
    NPAIR = B // 2
    assert 2 * NP == PART and B * NP == 512 and T == 512 and KC == 2
    FIRST = [0] + [GB + EB * e for e in range(E)]
    COUNT = [GB] + [EB] * E
    COLS = [slice(f * PART, (f + n) * PART) for f, n in zip(FIRST, COUNT)]
    NG = 1 + E
    GROUP_OF = [g for g in range(NG) for _ in range(COUNT[g])]
    LAG = 2
    SLOTS = B * NB

    es = ExitStack()
    with es:
        def sb(name, shape, dt=F32):
            return es.enter_context(nc.sbuf_tensor(name, shape, dt))

        def sem(name):
            return es.enter_context(nc.semaphore(name))

        XBUFS = 3
        xbuf = sb("xbuf", [PART, XBUFS, NT, H])
        w1n = sb("w1n", [PART, 2, KC, NCOL], F32R)
        w1v = sb("w1v", [PART, KC, NCOL])
        STAGES = 3
        stage = sb("stage", [PART, STAGES, KC, 512])
        work = sb("work", [PART, 5120])
        vw_pair = sb("vw_pair", [PART, 2, NCOL], F32R)
        vw = sb("vw", [PART, 2, NCOL], F32R)
        w2 = sb("w2", [PART, 2, E * EB, H], F32R)
        gw2 = sb("gw2", [PART, 2, GB, H], F32R)
        qk = sb("qk", [PART, 2, KC, B * NP], F32R)
        vT = sb("vT", [PART, KC, B * NP])
        HRING = 3
        h = sb("h", [PART, HRING, 2, T], F32R)
        hf = sb("hf", [PART, 2, T])
        nx = sb("nx", [PART, 2, 2, KC, T], F32R)
        xw = sb("xw", [PART, NT * H])
        xhat = xw[:, :].rearrange("p (t h) -> p t h", t=NT)
        nxf = xw[:, :].rearrange("p (k t) -> p k t", k=KC)
        sm_d = sb("sm_d", [PART, NT, NP])
        sm_e = sb("sm_e", [PART, NT, NP])
        wcat = sb("wcat", [PART, NT, 2, NP], F32R)
        wT = sb("wT", [PART, 2, T], F32R)
        b2o = sb("b2o", [PART, E, H])
        outb_bc = sb("outb_bc", [PART, H])
        gb2_bc = sb("gb2_bc", [PART, H])
        ident = sb("ident", [PART, PART])
        ones8 = sb("ones8", [8, PART])
        NROWS = NB + 2 * KC + E * KC + B * KC
        rows = hf[0:NROWS, 0, 0:PART]
        gw2_raw = hf[:, 1, :].rearrange("p (k n) -> p k n", k=GB)
        cols = sb("cols", [PART, NROWS])
        C_B1, C_GAMMA, C_BETA = 0, NB, NB + KC
        C_B2 = C_BETA + KC
        C_COND = C_B2 + E * KC
        zb = sb("zb", [PART, NB, B])
        wr = sb("wr", [PART, 3 * KC, RP])
        wrn = sb("wrn", [PART, 2, KC, RP], F32R)
        vwr_f = sb("vwr_f", [PART, B, RP])
        vwr = sb("vwr", [PART, 2, B, RP], F32R)
        rb_bc = sb("rb_bc", [8, E])
        lb = sb("lb", [8, RP])
        lb_diag = sb("lb_diag", [8, B, RP])
        lb_bc = sb("lb_bc", [PART, B, RP])
        stats = sb("stats", [PART, NT, 6])
        mv = sb("mv", [PART, NT, 2])
        ve = sb("ve", [PART, NT])
        rstd = sb("rstd", [PART, NT])
        minus_half = sb("minus_half", [PART, NT])
        red = sb("red", [PART, 3, NT])
        red3 = sb("red3", [PART, 4, NT])
        lg = sb("lg", [PART, NT, RP])
        lgd = sb("lgd", [PART, NT, RP])
        lge = sb("lge", [PART, NT, RP])
        ph = sb("ph", [PART, 2, NT, RP])
        ctx_raw = work[:, 0:1024].rearrange("p (t h) -> p t h", t=4)
        pT = work[:, 1024:2048].rearrange("p (k n) -> p k n", k=KC)
        kT = work[:, 2048:3072].rearrange("p (k n) -> p k n", k=KC)
        wv_raw = work[:, 3072:3584].rearrange("p (k n) -> p k n", k=KC)
        wq_raw = work[:, 3584:4096].rearrange("p (k n) -> p k n", k=KC)
        wk_raw = work[:, 4096:4608].rearrange("p (k n) -> p k n", k=KC)
        wqT = work[:, 4608:5120].rearrange("p (k n) -> p k n", k=KC)
        acc = work[:, 0:1024].rearrange("p (t h) -> p t h", t=NT)
        tg = work[:, 1024:2048].rearrange("p (t h) -> p t h", t=NT)
        bsum = work[:, 2048:3072].rearrange("p (t h) -> p t h", t=NT)
        btmp = work[:, 3072:3584].rearrange("p (i h) -> p i h", i=2)
        ow_raw = work[:, 3584:4096].rearrange("p (k n) -> p k n", k=KC)
        b2_bc = work[:, 4096:4096 + E * KC * PART].rearrange("p (c n) -> p c n", n=PART)
        ewT = work[:, 4096:5120].rearrange("p (k n) -> p k n", k=KC)

        bank = [es.enter_context(nc.psum_tensor(f"bank{i}", [PART, 512], F32)) for i in range(8)]
        ZB, AB, MB = (0, 1, 2), (3, 4, 5), (6, 7)

        s_x = [sem(f"s_x{i}") for i in range(XBUFS)]
        s_rows, s_ctx, s_wk, s_wq, s_wv = (sem(n) for n in ("s_rows", "s_ctx", "s_wk", "s_wq", "s_wv"))
        s_wr, s_bc, s_ow, s_gw2 = (sem(n) for n in ("s_wr", "s_bc", "s_ow", "s_gw2"))
        s_w1v = [sem(f"s_w1v{c}") for c in range(NG)]
        s_stage = [sem(f"s_stage{i}") for i in range(STAGES)]
        s_dup = [sem(f"s_dup{c}") for c in range(NG)]
        s_out = sem("s_out")
        s_pool0 = sem("s_pool0")
        s_prep = sem("s_prep")
        s_pv = sem("s_pv")
        s_pa = sem("s_pa")
        s_w1hi, s_w1lo = sem("s_w1hi"), sem("s_w1lo")
        s_gwhi, s_gwlo = sem("s_gwhi"), sem("s_gwlo")
        s_zbc = sem("s_zbc")
        s_vwp, s_phi, s_plo = sem("s_vwp"), sem("s_phi"), sem("s_plo")
        s_ewT, s_ewc = sem("s_ewT"), sem("s_ewc")
        s_fold, s_fhi, s_flo = sem("s_fold"), sem("s_fhi"), sem("s_flo")
        s_ve, s_rstd, s_xhat = sem("s_ve"), sem("s_rstd"), sem("s_xhat")
        s_xT, s_nf, s_nhi, s_nlo = sem("s_xT"), sem("s_nf"), sem("s_nhi"), sem("s_nlo")
        s_sc, s_d, s_e, s_wc, s_wt, s_wT = (sem(n) for n in ("s_sc", "s_d", "s_e", "s_wc", "s_wt", "s_wT"))
        s_lg, s_lgin, s_d3, s_e3, s_ph = (sem(n) for n in ("s_lg", "s_lgin", "s_d3", "s_e3", "s_ph"))
        s_z = sem("s_z")
        s_h = sem("s_h")
        s_hlo = sem("s_hlo")
        s_w2 = sem("s_w2")
        s_acc = sem("s_acc")
        s_comb = sem("s_comb")
        s_tg = sem("s_tg")
        s_bs = sem("s_bs")
        s_y = sem("s_y")
        s_o = sem("s_o")
        s_vc, s_gc = sem("s_vc"), sem("s_gc")

        blk = es.enter_context(nc.Block())

        staged = [("n", 0), ("c", 0), ("n", 1), ("c", 1), ("n", 2), ("c", 2), ("n", 3), ("c", 3),
                  ("w2", 0), ("w2", 1), ("w2", 2)]
        assert NG == 4

        def stage_of(kind, g):
            u = staged.index((kind, g))
            return u % STAGES, (s_stage[u % STAGES], 16 * (u // STAGES + 1))

        def plan(engine, b, j, when):
            steps = []
            nxt, nxt2 = b + 1, b + 2
            if b == 0:
                at = {"ewT0": 0, "fold0": 1, "xT": 2, "ewT1": 3, "sc": 4, "fold1": 5, "wt": 6,
                      "ewT2": 7, "fold2": 8, "lg": 9}
            else:
                at = {"xT": 0, "sc": 2, "wt": 5, "lg": 8}
            if nxt >= B:
                at = {}
            elif b % 2 == 1:
                at |= {"vwp0": 1, "vwp1": 3, "vwp2": 6, "vwp3": 10}
            name = {j2: n for n, j2 in at.items()}
            now, before = name.get(j), name.get(j - 1)
            kind = (lambda n: n[:-1] if n and n[-1].isdigit() else n)
            arg = (lambda n: int(n[-1]))
            if engine == "pe" and when == "pre" and now:
                k = kind(now)
                steps.append((k, arg(now)) if k in ("ewT", "fold") else
                             (k, nxt // 2, arg(now)) if k == "vwp" else (k, nxt))
            if engine == "act":
                if when == "pre" and kind(now) == "ewT":
                    steps.append(("ew_copy", arg(now)))
                if when == "post":
                    if kind(now) == "fold":
                        steps.append(("fold_hi", arg(now)))
                    if now == "xT":
                        steps.append(("nx_hi", nxt))
                    if now == "sc":
                        steps.append(("exp", nxt))
                    if now == "wt":
                        steps.append(("wT_copy", nxt))
                    if now == "lg":
                        steps.append(("exp_router", nxt))
                    if kind(now) == "vwp":
                        steps.append(("pair_hi", nxt // 2, arg(now)))
                if when == "post" and j == GB + LAG:
                    steps.append(("gate_tanh", b))
            if engine == "dve":
                if when == "pre" and before == "xT":
                    steps.append(("nx_lo", nxt))
                if when == "post":
                    if now == "xT":
                        steps.append(("nx_full", nxt))
                    if now == "sc":
                        steps.append(("score_max", nxt))
                    if before == "sc":
                        steps.append(("weights", nxt))
                    if now == "lg":
                        steps.append(("router_max", nxt))
                    if before == "lg":
                        steps.append(("router_prob", nxt))
                    if kind(now) == "fold":
                        steps.append(("fold_lo", arg(now)))
                    if kind(now) == "vwp":
                        steps.append(("pair_lo", nxt // 2, arg(now)))
                    if j == 11 and nxt2 < B:
                        steps.append(("stats", nxt2))
                    if j == 12 and nxt2 < B:
                        steps.append(("normalise", nxt2))
            return steps

        def run_plan(steps, engine, b, j, when):
            for name, *args in plan(engine, b, j, when):
                steps[name](*args)

        PREP = {n: i + 1 for i, n in enumerate(
            ("cols", "pT0", "pT1", "wqT", "kT0", "kT1", "qk0", "qk1", "vT0", "vT1", "lb", "vwr", "lb_bc",
             "b2o01", "b2o2", "zb"))}
        PV = {n: i + 1 for i, n in enumerate(
            ("cols", "pT0", "wqT", "kT0", "qk0", "qk1", "b2_bc", "vT0", "lb", "vwr", "router_lo", "lb_bc", "b2o01", "b2o2",
             "zb"))}
        PA = {n: i + 1 for i, n in enumerate(("pT1", "kT1", "qk0", "qk1", "vT1"))}

        @blk.sync
        def _(sp):
            def load_x(b):
                sp.dma_start(xbuf[:, b % XBUFS, :, :], x[b].rearrange("(t p) h -> p t h", p=PART))\
                  .then_inc(s_x[b % XBUFS], 16)

            def first_layer(g, part):
                w = gate_w1 if g == 0 else e_w1[g - 1]
                return w[part * H:(part + 1) * H, :].rearrange("(k p) n -> p k n", p=PART)

            def load_w1v(g):
                sp.dma_start(w1v[:, :, COLS[g]], first_layer(g, 1)).then_inc(s_w1v[g], 16)

            def load_staged(kind, g):
                u = staged.index((kind, g))
                if u >= STAGES:
                    before, bg = staged[u - STAGES]
                    if before == "n":
                        sp.wait_ge(s_w1lo, bg + 1)
                    elif before == "c" and bg == NG - 1:
                        sp.wait_ge(s_prep, PREP["zb"])
                    elif before == "c":
                        sp.wait_ge(s_zbc, bg + 1)
                    else:
                        sp.wait_ge(s_ewT, bg + 1)
                if kind == "w2":
                    dst = stage[:, u % STAGES, :, :].rearrange("p k n -> p (k n)").rearrange(
                        "p (i h) -> p i h", h=H)
                    src = e_w2[g].rearrange("(i p) h -> p i h", p=PART)
                else:
                    dst = stage[:, u % STAGES, :, 0:COUNT[g] * PART]
                    src = first_layer(g, 0 if kind == "n" else 2)
                sp.dma_start(dst, src).then_inc(s_stage[u % STAGES], 16)

            def square(w):
                return w.rearrange("(k p) n -> p k n", p=PART)

            load_x(0)
            sp.dma_start(ctx_raw, ctx.rearrange("b q h -> (b q) h").rearrange("(t p) h -> p t h", p=PART))\
              .then_inc(s_ctx, 16)
            sp.dma_start(wk_raw, square(Wk)).then_inc(s_wk, 16)
            sp.dma_start(wq_raw, square(Wq)).then_inc(s_wq, 16)
            sp.dma_start(wv_raw, square(Wv)).then_inc(s_wv, 16)
            load_staged("n", 0)
            load_w1v(0)
            load_staged("c", 0)
            load_staged("n", 1)
            load_w1v(1)
            load_x(1)
            load_w1v(2)
            load_w1v(3)
            sp.wait_ge(s_prep, PREP["qk1"])
            sp.dma_start(ow_raw, square(out_w)).then_inc(s_ow, 16)
            load_staged("c", 1)
            load_staged("n", 2)
            load_staged("c", 2)
            load_staged("n", 3)
            load_staged("c", 3)
            sp.dma_start(gw2_raw, square(gate_w2)).then_inc(s_gw2, 16)
            load_x(2)

            def load_vw(b, g):
                sp.wait_ge(s_plo, NG * (b // 2) + g + 1)
                sp.wait_ge(s_phi, NG * (b // 2) + g + 1)
                if b >= 1:
                    sp.wait_ge(s_z, NB * (b - 1) + FIRST[g] + COUNT[g])
                r = NP * (b % 2)
                for half in range(2):
                    sp.dma_start(vw[NP * half:NP * (half + 1), :, COLS[g]].bitcast(F32),
                                 vw_pair[r:r + NP, :, COLS[g]].bitcast(F32)).then_inc(s_dup[g], 16)

            for g in range(NG):
                load_vw(0, g)
            for e in range(E):
                load_staged("w2", e)

            def store(b):
                sp.wait_ge(s_o, b + 1)
                sp.dma_start(out[b].rearrange("(t p) h -> p t h", p=PART), xbuf[:, b % XBUFS, :, :])\
                  .then_inc(s_out, 16)

            for b in range(B):
                for g in range(NG):
                    if b + 1 < B:
                        load_vw(b + 1, g)
                    if g == 0 and b >= 1:
                        store(b - 1)
                        if b + 2 < B:
                            sp.wait_ge(s_out, 16 * b)
                            load_x(b + 2)
            store(B - 1)
            sp.wait_ge(s_out, 16 * B)

        @blk.tensor
        def _(pe):
            readers = {}

            def take(i, last_reader=None):
                if i in readers:
                    pe.wait_ge(*readers[i])
                readers[i] = last_reader
                return bank[i]

            def split_product(dst, pairs, first=True, last=True):
                n = len(pairs) * len(SPLIT_PASSES)
                i = 0
                for lhs, rhs in pairs:
                    for a, c in SPLIT_PASSES:
                        mm = pe.matmul(dst, lhs(a), rhs(c), start=first and i == 0, stop=last and i == n - 1)
                        i += 1
                return mm

            def x_transpose(b):
                pe.wait_ge(s_xhat, b + 1)
                for k in range(KC):
                    dst = take(MB[k], (s_nf, KC * b + k + 1))
                    for t in range(NT):
                        mm = pe.transpose(dst[:, t * PART:(t + 1) * PART], xhat[:, t, k * PART:(k + 1) * PART],
                                          ident[:, :])
                mm.then_inc(s_xT, 1)

            def nx_lhs(b, k, t):
                return lambda part: nx[:, b % 2, part, k, t * PART:(t + 1) * PART]

            def scores(b):
                pe.wait_ge(s_nlo, KC * (b + 1))
                pe.wait_ge(s_nhi, KC * (b + 1))
                dst = take(MB[0], (s_d, b + 1))
                for t in range(NT):
                    mm = split_product(dst[:, t * NP:(t + 1) * NP],
                                       [(nx_lhs(b, k, t), lambda part, k=k: qk[:, part, k, b * NP:(b + 1) * NP])
                                        for k in range(KC)])
                mm.then_inc(s_sc, 1)

            def w_transpose(b):
                pe.wait_ge(s_wc, b + 1)
                dst = take(MB[1], (s_wT, b + 1))
                for t in range(NT):
                    mm = pe.transpose(dst[:, t * PART:(t + 1) * PART],
                                      wcat[:, t, :, :].rearrange("p a n -> p (a n)").bitcast(F32), ident[:, :])
                mm.then_inc(s_wt, 1)

            def logits(b):
                pe.wait_ge(s_wT, b + 1)
                dst = take(MB[1] if b > 1 else MB[0], (s_lgin, b + 1))
                for t in range(NT):
                    o = dst[:, t * RP:(t + 1) * RP]
                    split_product(o, [(nx_lhs(b, k, t), lambda part, k=k: wrn[:, part, k, :])
                                      for k in range(KC)], last=False)
                    for part in (HI, LO):
                        mm = pe.matmul(o, wT[:, b % 2, t * PART:(t + 1) * PART], vwr[:, part, b, :],
                                       start=False, stop=part == LO)
                mm.then_inc(s_lg, 1)

            def pair_product(pair, g, dst=None):
                pe.wait_ge(s_w1v[g], 16)
                done = (s_plo, NG * pair + g + 1)
                dst = take(dst if dst is not None else MB[1 - g % 2], done)
                n = COUNT[g] * PART
                for k in range(KC):
                    mm = pe.matmul(dst[:, 0:n], vT[:, k, pair * PART:(pair + 1) * PART], w1v[:, k, COLS[g]],
                                   start=k == 0, stop=k == KC - 1)
                mm.then_inc(s_vwp, 1)

            def w2_transpose(e):
                i, arrived = stage_of("w2", e)
                pe.wait_ge(*arrived)
                raw = stage[:, i, :, :].rearrange("p k n -> p (k n)").rearrange("p (i h) -> p i h", h=H)
                for k in range(KC):
                    dst = take(MB[k], (s_ewc, KC * e + k + 1))
                    for i in range(EB):
                        mm = pe.transpose(dst[:, i * PART:(i + 1) * PART], raw[:, i, k * PART:(k + 1) * PART],
                                          ident[:, :])
                mm.then_inc(s_ewT, 1)

            def w2_fold(e):
                pe.wait_ge(s_ewc, KC * (e + 1))
                pe.wait_ge(s_ow, 16)
                for i in range(EB):
                    if i % 2 == 0:
                        dst = take(MB[i // 2], (s_flo, 2 * e + i // 2 + 1))
                    for k in range(KC):
                        mm = pe.matmul(dst[:, (i % 2) * H:(i % 2 + 1) * H], ewT[:, k, i * PART:(i + 1) * PART],
                                       ow_raw[:, k, :], start=k == 0, stop=k == KC - 1)
                    if i % 2 == 1:
                        mm.then_inc(s_fold, 1)

            steps = {"xT": x_transpose, "sc": scores, "wt": w_transpose, "lg": logits, "vwp": pair_product,
                     "ewT": w2_transpose, "fold": w2_fold}

            done = 0

            def prep(name, mm):
                nonlocal done
                done += 1
                assert PREP[name] == done
                mm.then_inc(s_prep, 1)

            pe.wait_ge(s_pool0, 2)
            x_transpose(0)
            pe.wait_ge(s_rows, 96)
            prep("cols", pe.transpose(take(0, (s_pv, PV["cols"]))[:, 0:NROWS], rows,
                                      ident[0:NROWS, 0:NROWS]))
            pe.wait_ge(s_ctx, 16)
            for k in range(KC):
                dst = take(1 + k, (s_pv, PV["pT0"]) if k == 0 else (s_pa, PA["pT1"]))
                for t in range(4):
                    mm = pe.transpose(dst[:, t * PART:(t + 1) * PART], ctx_raw[:, t, k * PART:(k + 1) * PART],
                                      ident[:, :])
                prep(f"pT{k}", mm)
            pe.wait_ge(s_wq, 16)
            dst = take(3, (s_pv, PV["wqT"]))
            for j in range(KC):
                for i in range(KC):
                    mm = pe.transpose(dst[:, j * H + i * PART:j * H + (i + 1) * PART],
                                      wq_raw[:, i, j * PART:(j + 1) * PART], ident[:, :])
            prep("wqT", mm)

            def product(name, i, reader, lhs, rhs, n=B * NP, m=PART):
                dst = take(i, reader)
                for k in range(KC):
                    mm = pe.matmul(dst[0:m, 0:n], lhs(k), rhs(k), start=k == 0, stop=k == KC - 1)
                prep(name, mm)

            pe.wait_ge(s_wk, 16)
            pe.wait_ge(s_pv, PV["pT0"])
            pe.wait_ge(s_pa, PA["pT1"])
            for j in range(KC):
                product(f"kT{j}", 4 + j, (s_pv, PV["kT0"]) if j == 0 else (s_pa, PA["kT1"]),
                        lambda k: wk_raw[:, k, j * PART:(j + 1) * PART], lambda k: pT[:, k, :])
            pe.wait_ge(s_pv, PV["kT0"])
            pe.wait_ge(s_pa, PA["kT1"])
            for i in range(KC):
                product(f"qk{i}", i, (s_pv, PV[f"qk{i}"]),
                        lambda j: wqT[:, j, i * PART:(i + 1) * PART], lambda j: kT[:, j, :])
            pe.wait_ge(s_wv, 16)
            for j in range(KC):
                product(f"vT{j}", 2 + j, (s_pv, PV["vT0"]) if j == 0 else (s_pa, PA["vT1"]),
                        lambda k: wv_raw[:, k, j * PART:(j + 1) * PART], lambda k: pT[:, k, :])
            pe.wait_ge(s_pv, PV["qk1"])
            scores(0)
            pe.wait_ge(s_wr, 32)
            product("lb", 4, (s_pv, PV["lb"]), lambda k: cols[:, C_COND + k:C_COND + B * KC:KC],
                    lambda k: wr[:, 2 * KC + k, :], n=RP, m=B)
            pe.wait_ge(s_pv, PV["vT0"])
            pe.wait_ge(s_pa, PA["vT1"])
            dst = take(5, (s_pv, PV["vwr"]))
            for pair in range(NPAIR):
                for k in range(KC):
                    mm = pe.matmul(dst[:, pair * RP:(pair + 1) * RP], vT[:, k, pair * PART:(pair + 1) * PART],
                                   wr[:, KC + k, :], start=k == 0, stop=k == KC - 1)
            prep("vwr", mm)
            for g in range(NG):
                pair_product(0, g, dst=(0, 1, 2, 3)[g])
            pe.wait_ge(s_pv, PV["lb"])
            prep("lb_bc", pe.matmul(take(4, (s_pv, PV["lb_bc"]))[:, 0:B * RP], ones8[:, :],
                                    lb_diag[:, :, :].rearrange("p b c -> p (b c)"), start=True, stop=True))
            w_transpose(0)
            pe.wait_ge(s_pv, PV["router_lo"])
            logits(0)
            pe.wait_ge(s_ow, 16)
            pe.wait_ge(s_pv, PV["b2_bc"])
            dst = take(5, (s_pv, PV["b2o01"]))
            for e in range(E):
                if e == 2:
                    prep("b2o01", mm)
                    dst = take(0, (s_pv, PV["b2o2"]))
                for k in range(KC):
                    mm = pe.matmul(dst[:, (e % 2) * H:(e % 2 + 1) * H], b2_bc[:, e * KC + k, :], ow_raw[:, k, :],
                                   start=k == 0, stop=k == KC - 1)
            prep("b2o2", mm)
            dst = take(1, (s_pv, PV["zb"]))
            for g in range(NG):
                i, arrived = stage_of("c", g)
                pe.wait_ge(*arrived)
                for c in range(COUNT[g]):
                    j = FIRST[g] + c
                    for k in range(KC):
                        mm = pe.matmul(dst[:, j * B:(j + 1) * B], stage[:, i, k, c * PART:(c + 1) * PART],
                                       cols[:, C_COND + k:C_COND + B * KC:KC], start=k == 0, stop=k == KC - 1)
                if g < NG - 1:
                    mm.then_inc(s_zbc, 1)
            prep("zb", mm)

            def first_layer(s):
                b, j = divmod(s, NB)
                g = GROUP_OF[j]
                if b == 0 and j == FIRST[g]:
                    pe.wait_ge(s_w1hi, g + 1)
                    pe.wait_ge(s_w1lo, g + 1)
                if j == 0:
                    pe.wait_ge(s_nlo, KC * (b + 1))
                    pe.wait_ge(s_nhi, KC * (b + 1))
                dst = take(ZB[s % 3], (s_h, 2 * (s + 1)))[:, :]
                blk_cols = slice(j * PART, (j + 1) * PART)
                split_product(dst, [(lambda part, k=k: w1n[:, part, k, blk_cols],
                                     lambda part, k=k: nx[:, b % 2, part, k, :]) for k in range(KC)], last=False)
                if j == 0:
                    pe.wait_ge(s_wT, b + 1)
                if j == FIRST[g]:
                    pe.wait_ge(s_dup[g], 32 * (b + 1))
                for part in (HI, LO):
                    mm = pe.matmul(dst, vw[:, part, blk_cols], wT[:, b % 2, :], start=False, stop=part == LO)
                mm.then_inc(s_z, 1)

            def second_layer(s):
                b, j = divmod(s, NB)
                g = GROUP_OF[j]
                c = j - FIRST[g]
                pe.wait_ge(s_hlo, s + 1)
                pe.wait_ge(s_h, 2 * (s + 1))
                if b == 0 and g == 0 and c == 0:
                    pe.wait_ge(s_gwhi, 1)
                    pe.wait_ge(s_gwlo, 1)
                if b == 0 and g > 0 and c % 2 == 0:
                    pe.wait_ge(s_flo, 2 * (g - 1) + c // 2 + 1)
                    pe.wait_ge(s_fhi, 2 * (g - 1) + c // 2 + 1)
                for half in range(2):
                    u = 2 * (NG * b + g) + half
                    if c == 0:
                        take(AB[u % 3], (s_comb, u + 1))
                    for t in (2 * half, 2 * half + 1):
                        o = bank[AB[u % 3]][:, (t % 2) * H:(t % 2 + 1) * H]
                        for i, (a, w) in enumerate(SPLIT_PASSES):
                            rhs = gw2[:, w, c, :] if g == 0 else w2[:, w, j - GB, :]
                            mm = pe.matmul(o, h[:, s % HRING, a, t * PART:(t + 1) * PART], rhs,
                                           start=c == 0 and i == 0 and t % 2 == 0,
                                           stop=c == COUNT[g] - 1 and i == 2 and t % 2 == 1,
                                           skip_group_check=True)
                    if half == 0 and c == COUNT[g] - 1:
                        mm.then_inc(s_acc, 1)
                if c == COUNT[g] - 1:
                    mm.then_inc(s_acc, 1)
                else:
                    mm.then_inc(s_w2, 1)

            for s in range(SLOTS + LAG):
                b, j = divmod(s, NB)
                if s < SLOTS:
                    run_plan(steps, "pe", b, j, "pre")
                    first_layer(s)
                if s >= LAG:
                    second_layer(s - LAG)

        def h_free(eng, s):
            b, j = divmod(s, NB)
            g = GROUP_OF[j]
            if j == FIRST[g] + COUNT[g] - 1:
                eng.wait_ge(s_acc, 2 * (NG * b + g + 1))
            else:
                eng.wait_ge(s_w2, s + 1 - (NG * b + g))

        @blk.scalar
        def _(act):
            r0 = 0
            for src in (gate_b1.rearrange("(r c) -> r c", c=PART), e_b1.rearrange("e (i c) -> (e i) c", c=PART),
                        ln_gamma.rearrange("(r c) -> r c", c=PART), ln_beta.rearrange("(r c) -> r c", c=PART),
                        e_b2.rearrange("e (i c) -> (e i) c", c=PART), cond.rearrange("b (i c) -> (b i) c", c=PART)):
                act.dma_start(rows[r0:r0 + src.shape[0], :], src).then_inc(s_rows, 16)
                r0 += src.shape[0]
            act.wait_ge(s_pool0, 3)
            act.dma_start(wr[:, :, 0:E], router_W.rearrange("(k p) e -> p k e", p=PART)).then_inc(s_wr, 16)
            act.dma_start(rb_bc[:, :], router_b.partition_broadcast(8)).then_inc(s_wr, 16)
            act.dma_start(outb_bc[:, :], out_b.partition_broadcast(PART)).then_inc(s_bc, 16)
            act.dma_start(gb2_bc[:, :], gate_b2.partition_broadcast(PART)).then_inc(s_bc, 16)

            def nx_hi(b):
                for k in range(KC):
                    act.wait_ge(s_nf, KC * b + k + 1)
                    if b >= 2 and k == 0:
                        act.wait_ge(s_z, NB * (b - 1))
                    act.copy(nx[:, b % 2, HI, k, :], nxf[:, k, :]).then_inc(s_nhi, 1)

            def exp(b):
                act.wait_ge(s_d, b + 1)
                if b >= 1:
                    act.wait_ge(s_wc, b)
                act.activation(sm_e[:, :, :], sm_d[:, :, :], ACT.Exp, scale=H ** -0.5).then_inc(s_e, 1)

            def wT_copy(b):
                act.wait_ge(s_wt, b + 1)
                if b >= 2:
                    act.wait_ge(s_z, NB * (b - 1))
                act.copy(wT[:, b % 2, :], bank[MB[1]][:, :]).then_inc(s_wT, 1)

            def exp_router(b):
                act.wait_ge(s_d3, b + 1)
                act.activation(lge[:, :, 0:E], lgd[:, :, 0:E], ACT.Exp).then_inc(s_e3, 1)

            def pair_hi(pair, g, src=None):
                act.wait_ge(s_vwp, NG * pair + g + 1)
                if pair >= 1:
                    act.wait_ge(s_dup[g], 32 * 2 * pair)
                src = bank[src if src is not None else MB[1 - g % 2]]
                act.copy(vw_pair[:, HI, COLS[g]], src[:, 0:COUNT[g] * PART]).then_inc(s_phi, 1)

            def ew_copy(e):
                act.wait_ge(s_ewT, e + 1)
                if e >= 1:
                    act.wait_ge(s_fold, 2 * e)
                for k in range(KC):
                    act.copy(ewT[:, k, :], bank[MB[k]][:, :]).then_inc(s_ewc, 1)

            def fold_hi(e):
                for i in range(2):
                    act.wait_ge(s_fold, 2 * e + i + 1)
                    act.copy(w2[:, HI, e * EB + 2 * i:e * EB + 2 * i + 2, :].rearrange("p i h -> p (i h)"),
                             bank[MB[i]][:, :]).then_inc(s_fhi, 1)

            def gate_tanh(b):
                act.wait_ge(s_comb, 2 * (NG * b + 1))
                act.activation(tg, tg, ACT.Tanh, scale=0.5).then_inc(s_tg, 1)

            steps = {"nx_hi": nx_hi, "exp": exp, "wT_copy": wT_copy, "exp_router": exp_router,
                     "pair_hi": pair_hi, "ew_copy": ew_copy, "fold_hi": fold_hi, "gate_tanh": gate_tanh}

            def prep(name, dst, i, wait=None):
                act.wait_ge(s_prep, PREP[name])
                act.copy(dst, bank[i][:, :]).then_inc(s_pa, 1)

            def w1_hi(g):
                i, arrived = stage_of("n", g)
                act.wait_ge(*arrived)
                act.copy(w1n[:, HI, :, COLS[g]], stage[:, i, :, 0:COUNT[g] * PART]).then_inc(s_w1hi, 1)

            prep("pT1", pT[:, 1, :], 2)
            nx_hi(0)
            prep("kT1", kT[:, 1, :], 5)
            prep("qk0", qk[:, HI, 0, :], 0)
            prep("qk1", qk[:, HI, 1, :], 1)
            prep("vT1", vT[:, 1, :], 3)
            exp(0)
            w1_hi(0)
            for g in range(NG):
                pair_hi(0, g, src=(0, 1, 2, 3)[g])
            w1_hi(1)
            wT_copy(0)
            exp_router(0)
            w1_hi(2)
            w1_hi(3)
            act.wait_ge(s_gw2, 16)
            act.copy(gw2[:, HI, :, :], gw2_raw).then_inc(s_gwhi, 1)

            for s in range(SLOTS):
                b, j = divmod(s, NB)
                run_plan(steps, "act", b, j, "pre")
                if s == 0:
                    act.wait_ge(s_pv, PV["zb"])
                if s == 1:
                    act.wait_ge(s_gwlo, 1)
                act.wait_ge(s_z, s + 1)
                if s >= 2:
                    act.wait_ge(s_hlo, s - 1)
                z = bank[ZB[s % 3]][:, :]
                act.activation(hf[:, s % 2, :], z, ACT.Silu, bias=zb[:, j, b:b + 1]).then_inc(s_h, 1)
                if s >= HRING:
                    h_free(act, s - HRING)
                act.activation(h[:, s % HRING, HI, :], z, ACT.Silu, bias=zb[:, j, b:b + 1]).then_inc(s_h, 1)
                run_plan(steps, "act", b, j, "post")

        @blk.vector
        def _(dve):
            chain = 0

            def link(ins):
                nonlocal chain
                chain += 1
                ins.then_inc(s_vc, 1)
                dve.wait_ge(s_vc, chain)

            def stats_of(b):
                dve.wait_ge(s_x[b % XBUFS], 16 * (b // XBUFS + 1))
                for t in range(NT):
                    ins = dve.bn_stats(stats[:, t, :], xbuf[:, b % XBUFS, t, :])
                link(ins)
                for t in range(NT):
                    ins = dve.bn_aggr(mv[:, t, :], stats[:, t, :])
                link(ins)
                if b >= 1:
                    dve.wait_ge(s_rstd, b)
                dve.tensor_scalar(ve[:, :], mv[:, :, 1], LN_EPS, None, ALU.add).then_inc(s_ve, 1)

            def normalise(b):
                dve.wait_ge(s_rstd, b + 1)
                if b >= 1:
                    dve.wait_ge(s_nhi, KC * b)
                    dve.wait_ge(s_nlo, KC * b)
                for t in range(NT):
                    ins = dve.tensor_scalar(xhat[:, t, :], xbuf[:, b % XBUFS, t, :], mv[:, t, 0:1],
                                            rstd[:, t:t + 1], ALU.subtract, ALU.mult)
                ins.then_inc(s_xhat, 1)

            def nx_full(b):
                dve.wait_ge(s_xT, b + 1)
                for k in range(KC):
                    dve.tensor_scalar(nxf[:, k, :], bank[MB[k]][:, :], cols[:, C_GAMMA + k:C_GAMMA + k + 1],
                                      cols[:, C_BETA + k:C_BETA + k + 1], ALU.mult, ALU.add).then_inc(s_nf, 1)

            def nx_lo(b):
                if b >= 2:
                    dve.wait_ge(s_z, NB * (b - 1))
                for k in range(KC):
                    dve.wait_ge(s_nhi, KC * b + k + 1)
                    dve.tensor_tensor(nx[:, b % 2, LO, k, :], nxf[:, k, :],
                                      nx[:, b % 2, HI, k, :].bitcast(F32), ALU.subtract).then_inc(s_nlo, 1)

            def over_last(v, n):
                return v.unsqueeze(2).broadcast_to([PART, NT, n])

            def score_max(b):
                dve.wait_ge(s_sc, b + 1)
                if b >= 1:
                    dve.wait_ge(s_wc, b)
                s = bank[MB[0]][:, 0:NT * NP].rearrange("p (t n) -> p t n", t=NT)
                link(dve.tensor_reduce(red[:, 0, :], s, AX_X, ALU.max))
                dve.tensor_tensor(sm_d[:, :, :], s, over_last(red[:, 0, :], NP), ALU.subtract).then_inc(s_d, 1)

            def weights(b):
                dve.wait_ge(s_e, b + 1)
                link(dve.tensor_reduce(red[:, 1, :], sm_e[:, :, :], AX_X, ALU.add))
                link(dve.reciprocal(red[:, 2, :], red[:, 1, :]))
                link(dve.tensor_tensor(sm_d[:, :, :], sm_e[:, :, :], over_last(red[:, 2, :], NP), ALU.mult))
                if b >= 1:
                    dve.wait_ge(s_wt, b)
                link(dve.tensor_copy(wcat[:, :, HI, :], sm_d[:, :, :]))
                dve.tensor_tensor(wcat[:, :, LO, :], sm_d[:, :, :], wcat[:, :, HI, :].bitcast(F32),
                                  ALU.subtract).then_inc(s_wc, 1)

            def router_max(b):
                dve.wait_ge(s_lg, b + 1)
                src = bank[MB[1] if b > 1 else MB[0]][:, 0:NT * RP].rearrange("p (t c) -> p t c", t=NT)
                bias = lb_bc[:, b, :].unsqueeze(1).broadcast_to([PART, NT, RP])
                dve.tensor_tensor(lg[:, :, :], src, bias, ALU.add).then_inc(s_lgin, 1)
                dve.wait_ge(s_lgin, b + 1)
                link(dve.tensor_reduce(red3[:, 0, :], lg[:, :, 0:E], AX_X, ALU.max))
                if b >= 1:
                    dve.wait_ge(s_e3, b)
                dve.tensor_tensor(lgd[:, :, 0:E], lg[:, :, 0:E], over_last(red3[:, 0, :], E),
                                  ALU.subtract).then_inc(s_d3, 1)

            def router_prob(b):
                dve.wait_ge(s_e3, b + 1)
                link(dve.tensor_reduce(red3[:, 1, :], lge[:, :, 0:E], AX_X, ALU.add))
                link(dve.reciprocal(red3[:, 2, :], red3[:, 1, :]))
                link(dve.tensor_scalar(red3[:, 3, :], red3[:, 2, :], 0.5, None, ALU.mult))
                if b >= 2:
                    dve.wait_ge(s_bs, b - 1)
                dve.tensor_tensor(ph[:, b % 2, :, 0:E], lge[:, :, 0:E], over_last(red3[:, 3, :], E),
                                  ALU.mult).then_inc(s_ph, 1)

            def pair_lo(pair, g, src=None):
                dve.wait_ge(s_phi, NG * pair + g + 1)
                src = bank[src if src is not None else MB[1 - g % 2]]
                dve.tensor_tensor(vw_pair[:, LO, COLS[g]], src[:, 0:COUNT[g] * PART],
                                  vw_pair[:, HI, COLS[g]].bitcast(F32), ALU.subtract).then_inc(s_plo, 1)

            def fold_lo(e):
                for i in range(2):
                    dve.wait_ge(s_fhi, 2 * e + i + 1)
                    blocks = slice(e * EB + 2 * i, e * EB + 2 * i + 2)
                    dve.tensor_tensor(w2[:, LO, blocks, :].rearrange("p i h -> p (i h)"), bank[MB[i]][:, :],
                                      w2[:, HI, blocks, :].rearrange("p i h -> p (i h)").bitcast(F32),
                                      ALU.subtract).then_inc(s_flo, 1)

            steps = {"stats": stats_of, "normalise": normalise, "nx_full": nx_full, "nx_lo": nx_lo,
                     "score_max": score_max, "weights": weights, "router_max": router_max,
                     "router_prob": router_prob, "pair_lo": pair_lo, "fold_lo": fold_lo}

            done = 0

            def prep(name, ins):
                nonlocal done
                done += 1
                assert PV[name] == done
                ins.then_inc(s_pv, 1)

            def prep_copy(name, dst, i, n=512):
                dve.wait_ge(s_prep, PREP[name])
                prep(name, dve.tensor_copy(dst, bank[i][:, 0:n]))

            def w1_lo(g):
                i, _ = stage_of("n", g)
                dve.wait_ge(s_w1hi, g + 1)
                dve.tensor_tensor(w1n[:, LO, :, COLS[g]], stage[:, i, :, 0:COUNT[g] * PART],
                                  w1n[:, HI, :, COLS[g]].bitcast(F32), ALU.subtract).then_inc(s_w1lo, 1)

            dve.memset(ones8[:, :], 1.0)
            stats_of(0)
            normalise(0)
            prep_copy("cols", cols[:, :], 0, NROWS)
            prep_copy("pT0", pT[:, 0, :], 1)
            prep_copy("wqT", wqT.rearrange("p k n -> p (k n)"), 3)
            dve.wait_ge(s_pv, PV["cols"])
            nx_full(0)
            prep_copy("kT0", kT[:, 0, :], 4)
            nx_lo(0)
            for i in range(KC):
                dve.wait_ge(s_pa, PA[f"qk{i}"])
                prep(f"qk{i}", dve.tensor_tensor(qk[:, LO, i, :], bank[i][:, :], qk[:, HI, i, :].bitcast(F32),
                                                 ALU.subtract))
            prep("b2_bc", dve.tensor_copy(b2_bc[:, :, :], cols[:, C_B2:C_B2 + E * KC].unsqueeze(2)
                                          .broadcast_to([PART, E * KC, PART])))
            prep_copy("vT0", vT[:, 0, :], 2)
            score_max(0)
            weights(0)
            dve.wait_ge(s_prep, PREP["lb"])
            dve.wait_ge(s_wr, 32)
            link(dve.memset(lb[:, :], 0.0))
            link(dve.tensor_tensor(lb[:, 0:E], bank[4][0:8, 0:E], rb_bc[:, :], ALU.add))
            dve.wait_ge(s_pool0, 2)
            prep("lb", dve.tensor_tensor(lb_diag[:, :, :], ident[0:8, 0:B].unsqueeze(2).broadcast_to([8, B, RP]),
                                         lb[:, :].unsqueeze(1).broadcast_to([8, B, RP]), ALU.mult))
            dve.wait_ge(s_prep, PREP["vwr"])
            for odd in range(2):
                src = bank[5][NP * odd:NP * (odd + 1), 0:NPAIR * RP].rearrange("p (q c) -> p q c", c=RP)
                for half in range(2):
                    dst = vwr_f[NP * half:NP * (half + 1), :, :].rearrange("p (q o) c -> p q o c", o=2)
                    ins = dve.tensor_copy(dst[:, :, odd, :], src)
            prep("vwr", ins)
            dve.wait_ge(s_pv, PV["vwr"])
            link(dve.tensor_copy(vwr[:, HI, :, :], vwr_f[:, :, :]))
            link(dve.tensor_tensor(vwr[:, LO, :, :], vwr_f[:, :, :], vwr[:, HI, :, :].bitcast(F32), ALU.subtract))
            link(dve.tensor_copy(wrn[:, HI, :, :], wr[:, 0:KC, :]))
            prep("router_lo", dve.tensor_tensor(wrn[:, LO, :, :], wr[:, 0:KC, :], wrn[:, HI, :, :].bitcast(F32),
                                                ALU.subtract))
            w1_lo(0)
            for g in range(NG):
                pair_lo(0, g, src=(0, 1, 2, 3)[g])
            prep_copy("lb_bc", lb_bc[:, :, :].rearrange("p b c -> p (b c)"), 4, B * RP)
            dve.wait_ge(s_pv, PV["lb_bc"])
            w1_lo(1)
            router_max(0)
            router_prob(0)
            dve.wait_ge(s_bc, 32)
            dve.wait_ge(s_prep, PREP["b2o01"])
            prep("b2o01", dve.tensor_tensor(b2o[:, 0:2, :], bank[5][:, :].rearrange("p (e h) -> p e h", e=2),
                                            outb_bc[:, :].unsqueeze(1).broadcast_to([PART, 2, H]), ALU.add))
            dve.wait_ge(s_prep, PREP["b2o2"])
            prep("b2o2", dve.tensor_tensor(b2o[:, 2, :], bank[0][:, 0:H], outb_bc[:, :], ALU.add))
            w1_lo(2)
            w1_lo(3)
            dve.wait_ge(s_prep, PREP["zb"])
            prep("zb", dve.tensor_tensor(zb[:, :, :], bank[1][:, 0:NB * B].rearrange("p (j b) -> p j b", j=NB),
                                         cols[:, C_B1:C_B1 + NB].unsqueeze(2).broadcast_to([PART, NB, B]), ALU.add))
            dve.wait_ge(s_gwhi, 1)
            dve.tensor_tensor(gw2[:, LO, :, :], gw2_raw, gw2[:, HI, :, :].bitcast(F32), ALU.subtract)\
               .then_inc(s_gwlo, 1)
            stats_of(1)
            normalise(1)

            def combine(b, g):
                for half in range(2):
                    u = 2 * (NG * b + g) + half
                    dve.wait_ge(s_acc, u + 1)
                    src = bank[AB[u % 3]][:, :].rearrange("p (i h) -> p i h", i=2)
                    tiles = slice(2 * half, 2 * half + 2)
                    if g == 0:
                        if b >= 1:
                            dve.wait_ge(s_y, b)
                        dve.tensor_tensor(tg[:, tiles, :], src, gb2_bc[:, :].unsqueeze(1)
                                          .broadcast_to([PART, 2, H]), ALU.add).then_inc(s_comb, 1)
                        continue
                    if g == 1 and half == 0:
                        dve.wait_ge(s_bs, b + 1)
                        if b >= 1:
                            dve.wait_ge(s_o, b)
                    if g > 1:
                        dve.wait_ge(s_comb, u - 1)
                    for i in range(2):
                        t = 2 * half + i
                        ins = dve.scalar_tensor_tensor(acc[:, t, :], src[:, i, :], ph[:, b % 2, t, g - 1:g],
                                                       (bsum if g == 1 else acc)[:, t, :], ALU.mult, ALU.add)
                    ins.then_inc(s_comb, 1)

            def gated(b):
                dve.wait_ge(s_tg, b + 1)
                dve.wait_ge(s_comb, 2 * NG * (b + 1))
                dve.scalar_tensor_tensor(acc, tg, 1.0, acc, ALU.add, ALU.mult).then_inc(s_y, 1)

            for s in range(SLOTS + LAG):
                b, j = divmod(s, NB)
                if s < SLOTS:
                    run_plan(steps, "dve", b, j, "pre")
                    dve.wait_ge(s_h, 2 * (s + 1))
                    if s >= HRING:
                        h_free(dve, s - HRING)
                    dve.tensor_tensor(h[:, s % HRING, LO, :], hf[:, s % 2, :],
                                      h[:, s % HRING, HI, :].bitcast(F32), ALU.subtract).then_inc(s_hlo, 1)
                if s >= LAG:
                    b2, j2 = divmod(s - LAG, NB)
                    g = GROUP_OF[j2]
                    if j2 == FIRST[g] + COUNT[g] - 1:
                        combine(b2, g)
                        if g == NG - 1:
                            gated(b2)
                if s < SLOTS:
                    run_plan(steps, "dve", b, j, "post")

        @blk.gpsimd
        def _(pool):
            chain = 0

            def link(ins):
                nonlocal chain
                chain += 1
                ins.then_inc(s_gc, 1)
                pool.wait_ge(s_gc, chain)

            def reciprocal_std(b):
                pool.wait_ge(s_ve, b + 1)
                if b >= 1:
                    pool.wait_ge(s_xhat, b)
                pool.tensor_tensor(rstd[:, :], ve[:, :], minus_half[:, :], ALU.pow).then_inc(s_rstd, 1)

            def bias_sum(b):
                pool.wait_ge(s_ph, b + 1)
                pool.wait_ge(s_pv, PV["b2o2"])
                if b >= 1:
                    pool.wait_ge(s_comb, 2 * (NG * (b - 1) + 2))
                for t in range(NT):
                    p = ph[:, b % 2, t, :]
                    pool.tensor_scalar(bsum[:, t, :], b2o[:, 0, :], p[:, 0:1], 0.0, ALU.mult, ALU.add)
                    for e in (1, 2):
                        ins = pool.tensor_scalar(btmp[:, e - 1, :], b2o[:, e, :], p[:, e:e + 1], 0.0,
                                                 ALU.mult, ALU.add)
                    link(ins)
                    link(pool.tensor_tensor(bsum[:, t, :], bsum[:, t, :], btmp[:, 0, :], ALU.add))
                    ins = pool.tensor_tensor(bsum[:, t, :], bsum[:, t, :], btmp[:, 1, :], ALU.add)
                    if t < NT - 1:
                        link(ins)
                ins.then_inc(s_bs, 1)

            pool.memset(minus_half[:, :], -0.5)
            pool.memset(ident[:, :], 0.0).then_inc(s_pool0, 1)
            pool.wait_ge(s_pool0, 1)
            pool.affine_select(out=ident[:, :], in_=ident[:, :], compare_op=ALU.not_equal, fill=1.0, base=0,
                               pattern=[[-1, PART]], channel_multiplier=1).then_inc(s_pool0, 1)
            pool.memset(wr[:, :, :], 0.0).then_inc(s_pool0, 1)
            reciprocal_std(0)
            reciprocal_std(1)
            bias_sum(0)
            for b in range(B):
                if b + 1 < B:
                    if b >= 1:
                        pass
                if b >= 1:
                    pool.wait_ge(s_y, b)
                    pool.tensor_tensor(xbuf[:, (b - 1) % XBUFS, :, :], xbuf[:, (b - 1) % XBUFS, :, :], acc,
                                       ALU.add).then_inc(s_o, 1)
                if b + 1 < B:
                    bias_sum(b + 1)
                if b + 2 < B:
                    reciprocal_std(b + 2)
            pool.wait_ge(s_y, B)
            pool.tensor_tensor(xbuf[:, (B - 1) % XBUFS, :, :], xbuf[:, (B - 1) % XBUFS, :, :], acc,
                               ALU.add).then_inc(s_o, 1)


_INS = ["x", "cond_1024", "ctx_1024", "L0_xcond_ln_gamma", "L0_xcond_ln_beta", "L0_xcond_Wq", "L0_xcond_Wk",
        "L0_xcond_Wv", "L0_xcond_router_W", "L0_xcond_router_b", "L0_xcond_e_w1", "L0_xcond_e_b1",
        "L0_xcond_e_w2", "L0_xcond_e_b2", "L0_xcond_gate_w1", "L0_xcond_gate_b1", "L0_xcond_gate_w2",
        "L0_xcond_gate_b2", "L0_xcond_out_w", "L0_xcond_out_b"]


def kernel(**inputs):
    import numpy as _np
    import concourse.bacc as _bacc
    from concourse import mybir as _mybir
    from concourse.bass_utils import run_bass_kernel_spmd as _run

    nc = _bacc.Bacc("TRN2", target_bir_lowering=False, num_devices=1)
    arrays, args = {}, []
    for name in _INS:
        a = _np.ascontiguousarray(inputs[name])
        arrays[f"in_{name}_dram"] = a
        args.append(nc.dram_tensor(f"in_{name}_dram", a.shape, _mybir.dt.from_np(a.dtype), kind="ExternalInput").ap())
    shape = tuple(inputs["x"].shape)
    args.append(nc.dram_tensor("out_0_dram", shape, _mybir.dt.float32, kind="ExternalOutput").ap())
    build(nc, *args)
    r = _run(nc, [arrays], core_ids=[0])
    return r.results[0]["out_0_dram"]
```

```python
from contextlib import ExitStack

import concourse.bass as bass
from concourse import mybir

F32 = mybir.dt.float32
F32R = mybir.dt.float32r
ALU = mybir.AluOpType
ACT = mybir.ActivationFunctionType
AX_X = mybir.AxisListType.X

PART = 128
LN_EPS = 1e-05
SPLIT_PASSES = ((0, 0), (0, 1), (1, 0))
HI, LO = 0, 1


def build(nc, x, cond, ctx, ln_gamma, ln_beta, Wq, Wk, Wv, router_W, router_b,
          e_w1, e_b1, e_w2, e_b2, gate_w1, gate_b1, gate_w2, gate_b2, out_w, out_b, out):
    B, T, H = x.shape
    NP = ctx.shape[1]
    E, _, R = e_w1.shape
    KC = H // PART
    NT = T // PART
    GB = H // PART
    EB = R // PART
    NB = GB + E * EB
    NCOL = NB * PART
    RP = 4
    NPAIR = B // 2
    assert 2 * NP == PART and B * NP == 512 and T == 512 and KC == 2
    FIRST = [0] + [GB + EB * e for e in range(E)]
    COUNT = [GB] + [EB] * E
    COLS = [slice(f * PART, (f + n) * PART) for f, n in zip(FIRST, COUNT)]
    NG = 1 + E
    GROUP_OF = [g for g in range(NG) for _ in range(COUNT[g])]
    STATS_SLOT = 8
    LAG = 2
    SLOTS = B * NB

    es = ExitStack()
    with es:
        def sb(name, shape, dt=F32):
            return es.enter_context(nc.sbuf_tensor(name, shape, dt))

        def sem(name):
            return es.enter_context(nc.semaphore(name))

        XBUFS = 3
        xbuf = sb("xbuf", [PART, XBUFS, NT, H])
        w1n = sb("w1n", [PART, 2, KC, NCOL], F32R)
        w1v = sb("w1v", [PART, KC, NCOL])
        STAGES = 3
        stage = sb("stage", [PART, STAGES, KC, 512])
        work = sb("work", [PART, 5120])
        vw_pair = sb("vw_pair", [PART, 2, NCOL], F32R)
        vw = sb("vw", [PART, 2, NCOL], F32R)
        w2 = sb("w2", [PART, 2, E * EB, H], F32R)
        gw2 = sb("gw2", [PART, 2, GB, H], F32R)
        SC = NP + RP
        qkr = sb("qkr", [PART, 2, KC, B, SC], F32R)
        vT = sb("vT", [PART, KC, B * NP])
        HRING = 3
        h = sb("h", [PART, HRING, 2, T], F32R)
        hf = sb("hf", [PART, 2, T])
        nx = sb("nx", [PART, 2, 2, KC, T], F32R)
        xw = sb("xw", [PART, NT * H])
        xhat = xw[:, :].rearrange("p (t h) -> p t h", t=NT)
        nxf = xw[:, :].rearrange("p (k t) -> p k t", k=KC)
        sm_d = sb("sm_d", [PART, NT, NP])
        sm_e = sb("sm_e", [PART, NT, NP])
        wcat = sb("wcat", [PART, NT, 2, NP], F32R)
        wT = sb("wT", [PART, 2, T], F32R)
        b2o = sb("b2o", [PART, E, H])
        outb_bc = sb("outb_bc", [PART, H])
        gb2_bc = sb("gb2_bc", [PART, H])
        ident = sb("ident", [PART, PART])
        ident_r = sb("ident_r", [PART, PART], F32R)
        ones8 = sb("ones8", [8, PART])
        NROWS = NB + 2 * KC + E * KC + B * KC
        rows = hf[0:NROWS, 0, 0:PART]
        gw2_raw = hf[:, 1, :].rearrange("p (k n) -> p k n", k=GB)
        cols = sb("cols", [PART, NROWS])
        C_B1, C_GAMMA, C_BETA = 0, NB, NB + KC
        C_B2 = C_BETA + KC
        C_COND = C_B2 + E * KC
        zb = sb("zb", [PART, NB, B])
        wr = sb("wr", [PART, 3 * KC, RP])
        vwr_f = sb("vwr_f", [PART, B, RP])
        vwr = sb("vwr", [PART, 2, B, RP], F32R)
        rb_bc = sb("rb_bc", [8, E])
        lb = sb("lb", [8, RP])
        lb_diag = sb("lb_diag", [8, B, RP])
        lb_bc = sb("lb_bc", [PART, B, RP])
        stats = sb("stats", [PART, NT, 6])
        mv = sb("mv", [PART, NT, 2])
        ve = sb("ve", [PART, NT])
        rstd = sb("rstd", [PART, NT])
        minus_half = sb("minus_half", [PART, NT])
        red = sb("red", [PART, 3, NT])
        red3 = sb("red3", [PART, 4, NT])
        lgn = sb("lgn", [PART, NT, RP])
        lg = sb("lg", [PART, NT, RP])
        lgd = sb("lgd", [PART, NT, RP])
        lge = sb("lge", [PART, NT, RP])
        ph = sb("ph", [PART, 2, NT, RP])
        ctx_raw = work[:, 0:1024].rearrange("p (t h) -> p t h", t=4)
        pT = work[:, 1024:2048].rearrange("p (k n) -> p k n", k=KC)
        kT = work[:, 2048:3072].rearrange("p (k n) -> p k n", k=KC)
        wv_raw = work[:, 3072:3584].rearrange("p (k n) -> p k n", k=KC)
        wq_raw = work[:, 3584:4096].rearrange("p (k n) -> p k n", k=KC)
        wk_raw = work[:, 4096:4608].rearrange("p (k n) -> p k n", k=KC)
        wqT = work[:, 4608:5120].rearrange("p (k n) -> p k n", k=KC)
        acc = work[:, 0:1024].rearrange("p (t h) -> p t h", t=NT)
        tg = work[:, 1024:2048].rearrange("p (t h) -> p t h", t=NT)
        bsum = work[:, 2048:3072].rearrange("p (t h) -> p t h", t=NT)
        btmp = work[:, 3072:3584].rearrange("p (i h) -> p i h", i=2)
        ow_raw = work[:, 3584:4096].rearrange("p (k n) -> p k n", k=KC)
        b2_bc = work[:, 4096:4096 + E * KC * PART].rearrange("p (c n) -> p c n", n=PART)
        ewT = work[:, 4096:5120].rearrange("p (k n) -> p k n", k=KC)

        bank = [es.enter_context(nc.psum_tensor(f"bank{i}", [PART, 512], F32)) for i in range(8)]
        PAIR_BANK = (7, 6, 7, 6)
        ZBIAS_BANK = (4, 5, 6, 7)
        ZB, AB, MB = (0, 1, 2), (3, 4, 5), (6, 7)

        s_x = [sem(f"s_x{i}") for i in range(XBUFS)]
        s_rows, s_ctx, s_wk, s_wq, s_wv = (sem(n) for n in ("s_rows", "s_ctx", "s_wk", "s_wq", "s_wv"))
        s_wr, s_bc, s_ow, s_gw2 = (sem(n) for n in ("s_wr", "s_bc", "s_ow", "s_gw2"))
        s_w1v = [sem(f"s_w1v{c}") for c in range(NG)]
        s_stage = [sem(f"s_stage{i}") for i in range(STAGES)]
        s_dup = [sem(f"s_dup{c}") for c in range(NG)]
        s_out = sem("s_out")
        s_pool0 = sem("s_pool0")
        s_prep = sem("s_prep")
        s_pv = sem("s_pv")
        s_pa = sem("s_pa")
        s_w1hi, s_w1lo = sem("s_w1hi"), sem("s_w1lo")
        s_gwhi, s_gwlo = sem("s_gwhi"), sem("s_gwlo")
        s_zbc = sem("s_zbc")
        s_zb = sem("s_zb")
        s_b2p, s_b2o = sem("s_b2p"), sem("s_b2o")
        s_vwp, s_phi, s_plo = sem("s_vwp"), sem("s_phi"), sem("s_plo")
        s_ewT, s_ewc = sem("s_ewT"), sem("s_ewc")
        s_fold, s_fhi, s_flo = sem("s_fold"), sem("s_fhi"), sem("s_flo")
        s_ve, s_rstd, s_xhat = sem("s_ve"), sem("s_rstd"), sem("s_xhat")
        s_xT, s_nf, s_nhi, s_nlo = sem("s_xT"), sem("s_nf"), sem("s_nhi"), sem("s_nlo")
        s_sc, s_d, s_e, s_wc, s_wt, s_wT = (sem(n) for n in ("s_sc", "s_d", "s_e", "s_wc", "s_wt", "s_wT"))
        s_lg, s_lgin, s_d3, s_e3, s_ph = (sem(n) for n in ("s_lg", "s_lgin", "s_d3", "s_e3", "s_ph"))
        s_max, s_lgn = sem("s_max"), sem("s_lgn")
        s_z = sem("s_z")
        s_h = sem("s_h")
        s_hlo = sem("s_hlo")
        s_w2 = sem("s_w2")
        s_acc = sem("s_acc")
        s_comb = sem("s_comb")
        s_tg = sem("s_tg")
        s_bs = sem("s_bs")
        s_y = sem("s_y")
        s_o = sem("s_o")
        s_vc, s_gc = sem("s_vc"), sem("s_gc")

        blk = es.enter_context(nc.Block())

        staged = [("n", 0), ("c", 0), ("n", 1), ("c", 1), ("w2", 0), ("n", 2), ("c", 2), ("w2", 1),
                  ("n", 3), ("c", 3), ("w2", 2)]
        assert NG == 4

        def stage_of(kind, g):
            u = staged.index((kind, g))
            return u % STAGES, (s_stage[u % STAGES], 16 * (u // STAGES + 1))

        FIRST_PLAN = {0: ["b2o"], 1: ["ewT0"], 2: ["fold0", "split2"], 3: ["zb2", "vwp2"], 4: ["xT"], 5: ["ewT1"],
                      6: ["fold1", "split3"], 7: ["sc", "zb3"], 8: ["vwp3"], 9: ["wt"], 10: ["ewT2"],
                      11: ["fold2"], 12: ["lg"]}
        EVEN_PLAN = {0: ["xT"], 2: ["sc"], 5: ["wt"], 7: ["lg"]}
        ODD_PLAN = {0: ["xT"], 1: ["vwp0"], 2: ["sc"], 4: ["vwp1"], 5: ["wt"], 7: ["lg"], 8: ["vwp2"], 10: ["vwp3"]}

        def plan(engine, b, j, when):
            nxt = b + 1
            at = FIRST_PLAN if b == 0 else ODD_PLAN if b % 2 == 1 else EVEN_PLAN
            steps = []
            for now in at.get(j, ()) if nxt < B else ():
                name = now.rstrip("0123456789")
                n = int(now[len(name):] or 0)
                args, pre, post = {
                    "xT": ((nxt,), {"act": ["nx_hi"], "dve": ["nx_full", "nx_lo"]}, {}),
                    "sc": ((nxt,), {"act": ["exp"], "dve": ["score_max"]}, {"dve": ["weights"]}),
                    "wt": ((nxt,), {"act": ["wT_copy"]}, {}),
                    "lg": ((nxt,), {"act": ["exp_router"], "dve": ["router_max"]}, {"dve": ["router_prob"]}),
                    "vwp": (((b + 1) // 2, n), {"act": ["pair_hi"], "dve": ["pair_lo"]}, {}),
                    "ewT": ((n,), {"act": ["ew_copy"]}, {}),
                    "fold": ((n,), {"act": ["fold_hi"], "dve": ["fold_lo"]}, {}),
                    "zb": ((n,), {"dve": ["z_bias"]}, {}),
                    "b2o": ((), {"dve": ["b2_out"]}, {}),
                    "split": ((n,), {}, {"act": ["w1_hi"], "dve": ["w1_lo"]}),
                }[name]
                if engine == "pe":
                    steps += [(name, *args)] if when == "pre" and name != "split" else []
                else:
                    steps += [(f, *args) for f in (pre if when == "pre" else post).get(engine, [])]
            if when == "post" and engine == "act" and j == GB + LAG:
                steps.append(("gate_tanh", b))
            if when == "post" and engine == "dve":
                if b == 0 and j in (0, 2):
                    steps.append(("stats" if j == 0 else "normalise", 1))
                if b + 2 < B and j in (STATS_SLOT, STATS_SLOT + 2):
                    steps.append(("stats" if j == STATS_SLOT else "normalise", b + 2))
            return steps

        def run_plan(steps, engine, b, j, when):
            for name, *args in plan(engine, b, j, when):
                steps[name](*args)

        PREP = {n: i + 1 for i, n in enumerate(
            ("cols", "lb", "pT0", "pT1", "wqT", "lb_bc", "kT0", "kT1", "qk0", "qk1", "vT0", "vT1", "vwr"))}
        PV = {n: i + 1 for i, n in enumerate(
            ("cols", "lb", "pT0", "wqT", "lb_bc", "kT0", "qk0", "qk1", "wr_lo", "vT0", "vwr", "vwr_lo", "b2_bc"))}
        PA = {n: i + 1 for i, n in enumerate(("pT1", "kT1", "qk0", "qk1", "vT1"))}

        @blk.sync
        def _(sp):
            def load_x(b):
                sp.dma_start(xbuf[:, b % XBUFS, :, :], x[b].rearrange("(t p) h -> p t h", p=PART))\
                  .then_inc(s_x[b % XBUFS], 16)

            def first_layer(g, part):
                w = gate_w1 if g == 0 else e_w1[g - 1]
                return w[part * H:(part + 1) * H, :].rearrange("(k p) n -> p k n", p=PART)

            def load_w1v(g):
                sp.dma_start(w1v[:, :, COLS[g]], first_layer(g, 1)).then_inc(s_w1v[g], 16)

            def load_staged(kind, g):
                u = staged.index((kind, g))
                if u >= STAGES:
                    before, bg = staged[u - STAGES]
                    if before == "n":
                        sp.wait_ge(s_w1lo, bg + 1)
                    elif before == "c":
                        sp.wait_ge(s_zbc, bg + 1)
                    else:
                        sp.wait_ge(s_ewT, bg + 1)
                if kind == "w2":
                    dst = stage[:, u % STAGES, :, :].rearrange("p k n -> p (k n)").rearrange(
                        "p (i h) -> p i h", h=H)
                    src = e_w2[g].rearrange("(i p) h -> p i h", p=PART)
                else:
                    dst = stage[:, u % STAGES, :, 0:COUNT[g] * PART]
                    src = first_layer(g, 0 if kind == "n" else 2)
                sp.dma_start(dst, src).then_inc(s_stage[u % STAGES], 16)

            def square(w):
                return w.rearrange("(k p) n -> p k n", p=PART)

            def load_vw(b, g):
                sp.wait_ge(s_plo, NG * (b // 2) + g + 1)
                sp.wait_ge(s_phi, NG * (b // 2) + g + 1)
                if b >= 1:
                    sp.wait_ge(s_z, NB * (b - 1) + FIRST[g] + COUNT[g])
                r = NP * (b % 2)
                for half in range(2):
                    sp.dma_start(vw[NP * half:NP * (half + 1), :, COLS[g]].bitcast(F32),
                                 vw_pair[r:r + NP, :, COLS[g]].bitcast(F32)).then_inc(s_dup[g], 16)

            sp.dma_start(ctx_raw, ctx.rearrange("b q h -> (b q) h").rearrange("(t p) h -> p t h", p=PART))\
              .then_inc(s_ctx, 16)
            sp.dma_start(wk_raw, square(Wk)).then_inc(s_wk, 16)
            load_x(0)
            sp.dma_start(wq_raw, square(Wq)).then_inc(s_wq, 16)
            sp.dma_start(wv_raw, square(Wv)).then_inc(s_wv, 16)
            load_staged("n", 0)
            load_w1v(0)
            load_staged("c", 0)
            load_staged("n", 1)
            load_w1v(1)
            load_x(1)
            sp.wait_ge(s_prep, PREP["wqT"])
            sp.dma_start(ow_raw, square(out_w)).then_inc(s_ow, 16)
            load_w1v(2)
            load_w1v(3)
            load_staged("c", 1)
            load_staged("w2", 0)
            load_vw(0, 0)
            load_vw(0, 1)
            load_staged("n", 2)
            load_staged("c", 2)
            load_x(2)
            load_vw(0, 2)
            load_staged("w2", 1)
            load_staged("n", 3)
            load_staged("c", 3)
            load_vw(0, 3)
            load_staged("w2", 2)

            def store(b):
                sp.wait_ge(s_o, b + 1)
                sp.dma_start(out[b].rearrange("(t p) h -> p t h", p=PART), xbuf[:, b % XBUFS, :, :])\
                  .then_inc(s_out, 16)

            for b in range(B):
                for g in range(NG):
                    if b + 1 < B:
                        load_vw(b + 1, g)
                    if g == 0 and b >= 1:
                        store(b - 1)
                        if b + 2 < B:
                            sp.wait_ge(s_out, 16 * b)
                            load_x(b + 2)
            store(B - 1)
            sp.wait_ge(s_out, 16 * B)

        @blk.tensor
        def _(pe):
            readers = {}

            def take(i, last_reader=None):
                if i in readers:
                    pe.wait_ge(*readers[i])
                readers[i] = last_reader
                return bank[i]

            def split_product(dst, pairs, first=True, last=True):
                n = len(pairs) * len(SPLIT_PASSES)
                i = 0
                for lhs, rhs in pairs:
                    for a, c in SPLIT_PASSES:
                        mm = pe.matmul(dst, lhs(a), rhs(c), start=first and i == 0, stop=last and i == n - 1)
                        i += 1
                return mm

            def x_transpose(b):
                pe.wait_ge(s_xhat, b + 1)
                for k in range(KC):
                    dst = take(MB[k], (s_nf, KC * b + k + 1))
                    for t in range(NT):
                        mm = pe.transpose(dst[:, t * PART:(t + 1) * PART], xhat[:, t, k * PART:(k + 1) * PART],
                                          ident[:, :])
                mm.then_inc(s_xT, 1)

            def nx_lhs(b, k, t):
                return lambda part: nx[:, b % 2, part, k, t * PART:(t + 1) * PART]

            def scores(b):
                pe.wait_ge(s_nlo, KC * (b + 1))
                pe.wait_ge(s_nhi, KC * (b + 1))
                dst = take(MB[0], (s_d, b + 1))
                for t in range(NT):
                    mm = split_product(dst[:, t * SC:(t + 1) * SC],
                                       [(nx_lhs(b, k, t), lambda part, k=k: qkr[:, part, k, b, :])
                                        for k in range(KC)])
                mm.then_inc(s_sc, 1)

            def w_transpose(b):
                pe.wait_ge(s_wc, b + 1)
                if b == 0:
                    pe.wait_ge(s_pool0, 4)
                dst = take(MB[1], (s_wT, b + 1))
                for t in range(NT):
                    mm = pe.transpose(dst[:, t * PART:(t + 1) * PART].bitcast(F32R),
                                      wcat[:, t, :, :].rearrange("p a n -> p (a n)"), ident_r[:, :])
                mm.then_inc(s_wt, 1)

            def logits(b):
                pe.wait_ge(s_wT, b + 1)
                dst = take(MB[1], (s_lgin, b + 1))
                for t in range(NT):
                    for part in (HI, LO):
                        mm = pe.matmul(dst[:, t * RP:(t + 1) * RP], wT[:, b % 2, t * PART:(t + 1) * PART],
                                       vwr[:, part, b, :], start=part == HI, stop=part == LO)
                mm.then_inc(s_lg, 1)

            def pair_product(pair, g, dst=None):
                pe.wait_ge(s_w1v[g], 16)
                done = (s_plo, NG * pair + g + 1)
                dst = take(dst if dst is not None else PAIR_BANK[g], done)
                n = COUNT[g] * PART
                for k in range(KC):
                    mm = pe.matmul(dst[:, 0:n], vT[:, k, pair * PART:(pair + 1) * PART], w1v[:, k, COLS[g]],
                                   start=k == 0, stop=k == KC - 1)
                mm.then_inc(s_vwp, 1)

            def w2_transpose(e):
                i, arrived = stage_of("w2", e)
                pe.wait_ge(*arrived)
                raw = stage[:, i, :, :].rearrange("p k n -> p (k n)").rearrange("p (i h) -> p i h", h=H)
                for k in range(KC):
                    dst = take(MB[k], (s_ewc, KC * e + k + 1))
                    for i in range(EB):
                        mm = pe.transpose(dst[:, i * PART:(i + 1) * PART], raw[:, i, k * PART:(k + 1) * PART],
                                          ident[:, :])
                mm.then_inc(s_ewT, 1)

            def w2_fold(e):
                pe.wait_ge(s_ewc, KC * (e + 1))
                pe.wait_ge(s_ow, 16)
                for i in range(EB):
                    if i % 2 == 0:
                        dst = take(MB[i // 2], (s_flo, 2 * e + i // 2 + 1))
                    for k in range(KC):
                        mm = pe.matmul(dst[:, (i % 2) * H:(i % 2 + 1) * H], ewT[:, k, i * PART:(i + 1) * PART],
                                       ow_raw[:, k, :], start=k == 0, stop=k == KC - 1)
                    if i % 2 == 1:
                        mm.then_inc(s_fold, 1)

            def anchor_product(g):
                i, arrived = stage_of("c", g)
                pe.wait_ge(*arrived)
                dst = take(ZBIAS_BANK[g], (s_zb, g + 1))
                for c in range(COUNT[g]):
                    for k in range(KC):
                        mm = pe.matmul(dst[:, c * B:(c + 1) * B], stage[:, i, k, c * PART:(c + 1) * PART],
                                       cols[:, C_COND + k:C_COND + B * KC:KC], start=k == 0, stop=k == KC - 1)
                mm.then_inc(s_zbc, 1)

            def b2_product():
                pe.wait_ge(s_ow, 16)
                pe.wait_ge(s_pv, PV["b2_bc"])
                for e in range(E):
                    if e % 2 == 0:
                        dst = take(MB[e // 2], (s_b2o, e // 2 + 1))
                    for k in range(KC):
                        mm = pe.matmul(dst[:, (e % 2) * H:(e % 2 + 1) * H], b2_bc[:, e * KC + k, :],
                                       ow_raw[:, k, :], start=k == 0, stop=k == KC - 1)
                mm.then_inc(s_b2p, 1)

            steps = {"xT": x_transpose, "sc": scores, "wt": w_transpose, "lg": logits, "vwp": pair_product,
                     "ewT": w2_transpose, "fold": w2_fold, "zb": anchor_product, "b2o": b2_product}

            done = 0

            def prep(name, mm):
                nonlocal done
                done += 1
                assert PREP[name] == done
                mm.then_inc(s_prep, 1)

            def product(name, i, reader, lhs, rhs, n=B * NP, m=PART):
                dst = take(i, reader)
                for k in range(KC):
                    mm = pe.matmul(dst[0:m, 0:n], lhs(k), rhs(k), start=k == 0, stop=k == KC - 1)
                prep(name, mm)

            pe.wait_ge(s_pool0, 2)
            pe.wait_ge(s_rows, 96)
            prep("cols", pe.transpose(take(0, (s_pv, PV["cols"]))[:, 0:NROWS], rows,
                                      ident[0:NROWS, 0:NROWS]))
            pe.wait_ge(s_wr, 32)
            pe.wait_ge(s_pv, PV["cols"])
            product("lb", 3, (s_pv, PV["lb"]), lambda k: cols[:, C_COND + k:C_COND + B * KC:KC],
                    lambda k: wr[:, 2 * KC + k, :], n=RP, m=B)
            pe.wait_ge(s_ctx, 16)
            for k in range(KC):
                dst = take(1 + k, (s_pv, PV["pT0"]) if k == 0 else (s_pa, PA["pT1"]))
                for t in range(4):
                    mm = pe.transpose(dst[:, t * PART:(t + 1) * PART], ctx_raw[:, t, k * PART:(k + 1) * PART],
                                      ident[:, :])
                prep(f"pT{k}", mm)
            pe.wait_ge(s_wq, 16)
            dst = take(0, (s_pv, PV["wqT"]))
            for j in range(KC):
                for i in range(KC):
                    mm = pe.transpose(dst[:, j * H + i * PART:j * H + (i + 1) * PART],
                                      wq_raw[:, i, j * PART:(j + 1) * PART], ident[:, :])
            prep("wqT", mm)
            pe.wait_ge(s_pv, PV["lb"])
            prep("lb_bc", pe.matmul(take(3, (s_pv, PV["lb_bc"]))[:, 0:B * RP], ones8[:, :],
                                    lb_diag[:, :, :].rearrange("p b c -> p (b c)"), start=True, stop=True))
            pe.wait_ge(s_wk, 16)
            pe.wait_ge(s_pv, PV["pT0"])
            pe.wait_ge(s_pa, PA["pT1"])
            for j in range(KC):
                product(f"kT{j}", 4 + j, (s_pv, PV["kT0"]) if j == 0 else (s_pa, PA["kT1"]),
                        lambda k: wk_raw[:, k, j * PART:(j + 1) * PART], lambda k: pT[:, k, :])
            x_transpose(0)
            pe.wait_ge(s_pv, PV["kT0"])
            pe.wait_ge(s_pa, PA["kT1"])
            for i in range(KC):
                product(f"qk{i}", i, (s_pv, PV[f"qk{i}"]),
                        lambda j: wqT[:, j, i * PART:(i + 1) * PART], lambda j: kT[:, j, :])
            pe.wait_ge(s_wv, 16)
            for j in range(KC):
                product(f"vT{j}", 2 + j, (s_pv, PV["vT0"]) if j == 0 else (s_pa, PA["vT1"]),
                        lambda k: wv_raw[:, k, j * PART:(j + 1) * PART], lambda k: pT[:, k, :])
            pe.wait_ge(s_pv, PV["wr_lo"])
            scores(0)
            pe.wait_ge(s_pv, PV["vT0"])
            pe.wait_ge(s_pa, PA["vT1"])
            dst = take(5, (s_pv, PV["vwr"]))
            for pair in range(NPAIR):
                for k in range(KC):
                    mm = pe.matmul(dst[:, pair * RP:(pair + 1) * RP], vT[:, k, pair * PART:(pair + 1) * PART],
                                   wr[:, KC + k, :], start=k == 0, stop=k == KC - 1)
            prep("vwr", mm)
            anchor_product(0)
            pair_product(0, 0, dst=0)
            pair_product(0, 1, dst=1)
            w_transpose(0)
            anchor_product(1)
            pe.wait_ge(s_pv, PV["vwr_lo"])
            logits(0)

            def first_layer(s):
                b, j = divmod(s, NB)
                g = GROUP_OF[j]
                if b == 0 and j == FIRST[g]:
                    pe.wait_ge(s_w1hi, g + 1)
                    pe.wait_ge(s_w1lo, g + 1)
                if j == 0:
                    pe.wait_ge(s_nlo, KC * (b + 1))
                    pe.wait_ge(s_nhi, KC * (b + 1))
                dst = (bank[ZB[s % 3]] if s >= 3 else take(ZB[s % 3]))[:, :]
                blk_cols = slice(j * PART, (j + 1) * PART)
                split_product(dst, [(lambda part, k=k: w1n[:, part, k, blk_cols],
                                     lambda part, k=k: nx[:, b % 2, part, k, :]) for k in range(KC)], last=False)
                if j == 0:
                    pe.wait_ge(s_wT, b + 1)
                if j == FIRST[g]:
                    pe.wait_ge(s_dup[g], 32 * (b + 1))
                for part in (HI, LO):
                    mm = pe.matmul(dst, vw[:, part, blk_cols], wT[:, b % 2, :], start=False, stop=part == LO)
                mm.then_inc(s_z, 1)

            def second_layer(s):
                b, j = divmod(s, NB)
                g = GROUP_OF[j]
                c = j - FIRST[g]
                pe.wait_ge(s_hlo, s + 1)
                if b == 0 and g == 0 and c == 0:
                    pe.wait_ge(s_gwhi, 1)
                    pe.wait_ge(s_gwlo, 1)
                if b == 0 and g > 0 and c % 2 == 0:
                    pe.wait_ge(s_flo, 2 * (g - 1) + c // 2 + 1)
                    pe.wait_ge(s_fhi, 2 * (g - 1) + c // 2 + 1)
                for half in range(2):
                    u = 2 * (NG * b + g) + half
                    if c == 0:
                        take(AB[u % 3], (s_comb, u + 1))
                    for t in (2 * half, 2 * half + 1):
                        o = bank[AB[u % 3]][:, (t % 2) * H:(t % 2 + 1) * H]
                        for i, (a, w) in enumerate(SPLIT_PASSES):
                            rhs = gw2[:, w, c, :] if g == 0 else w2[:, w, j - GB, :]
                            mm = pe.matmul(o, h[:, s % HRING, a, t * PART:(t + 1) * PART], rhs,
                                           start=c == 0 and i == 0 and t % 2 == 0,
                                           stop=c == COUNT[g] - 1 and i == 2 and t % 2 == 1,
                                           skip_group_check=True)
                    if half == 0 and c == COUNT[g] - 1:
                        mm.then_inc(s_acc, 1)
                if c == COUNT[g] - 1:
                    mm.then_inc(s_acc, 1)
                else:
                    mm.then_inc(s_w2, 1)

            for s in range(SLOTS + LAG):
                b, j = divmod(s, NB)
                if s < SLOTS:
                    run_plan(steps, "pe", b, j, "pre")
                    first_layer(s)
                if s >= LAG:
                    second_layer(s - LAG)

        def h_free(eng, s):
            b, j = divmod(s, NB)
            g = GROUP_OF[j]
            if j == FIRST[g] + COUNT[g] - 1:
                eng.wait_ge(s_acc, 2 * (NG * b + g + 1))
            else:
                eng.wait_ge(s_w2, s + 1 - (NG * b + g))

        @blk.scalar
        def _(act):
            r0 = 0
            for src in (gate_b1.rearrange("(r c) -> r c", c=PART), e_b1.rearrange("e (i c) -> (e i) c", c=PART),
                        ln_gamma.rearrange("(r c) -> r c", c=PART), ln_beta.rearrange("(r c) -> r c", c=PART),
                        e_b2.rearrange("e (i c) -> (e i) c", c=PART), cond.rearrange("b (i c) -> (b i) c", c=PART)):
                act.dma_start(rows[r0:r0 + src.shape[0], :], src).then_inc(s_rows, 16)
                r0 += src.shape[0]
            act.wait_ge(s_pool0, 3)
            act.dma_start(wr[:, :, 0:E], router_W.rearrange("(k p) e -> p k e", p=PART)).then_inc(s_wr, 16)
            act.dma_start(rb_bc[:, :], router_b.partition_broadcast(8)).then_inc(s_wr, 16)
            act.dma_start(gw2_raw, gate_w2.rearrange("(k p) n -> p k n", p=PART)).then_inc(s_gw2, 16)
            act.dma_start(outb_bc[:, :], out_b.partition_broadcast(PART)).then_inc(s_bc, 16)
            act.dma_start(gb2_bc[:, :], gate_b2.partition_broadcast(PART)).then_inc(s_bc, 16)

            def nx_hi(b):
                for k in range(KC):
                    act.wait_ge(s_nf, KC * b + k + 1)
                    if b >= 2 and k == 0:
                        act.wait_ge(s_z, NB * (b - 1))
                    act.copy(nx[:, b % 2, HI, k, :], nxf[:, k, :]).then_inc(s_nhi, 1)

            def exp(b):
                act.wait_ge(s_d, b + 1)
                if b >= 1:
                    act.wait_ge(s_wc, b)
                act.activation(sm_e[:, :, :], sm_d[:, :, :], ACT.Exp, scale=H ** -0.5).then_inc(s_e, 1)

            def wT_copy(b):
                act.wait_ge(s_wt, b + 1)
                if b >= 2:
                    act.wait_ge(s_z, NB * (b - 1))
                act.copy(wT[:, b % 2, :], bank[MB[1]][:, :]).then_inc(s_wT, 1)

            def exp_router(b):
                act.wait_ge(s_d3, b + 1)
                act.activation(lge[:, :, 0:E], lgd[:, :, 0:E], ACT.Exp).then_inc(s_e3, 1)

            def pair_hi(pair, g, src=None):
                act.wait_ge(s_vwp, NG * pair + g + 1)
                if pair >= 1:
                    act.wait_ge(s_dup[g], 32 * 2 * pair)
                src = bank[src if src is not None else PAIR_BANK[g]]
                act.copy(vw_pair[:, HI, COLS[g]], src[:, 0:COUNT[g] * PART]).then_inc(s_phi, 1)

            def ew_copy(e):
                act.wait_ge(s_ewT, e + 1)
                if e >= 1:
                    act.wait_ge(s_fold, 2 * e)
                else:
                    act.wait_ge(s_b2p, 1)
                for k in range(KC):
                    act.copy(ewT[:, k, :], bank[MB[k]][:, :]).then_inc(s_ewc, 1)

            def fold_hi(e):
                for i in range(2):
                    act.wait_ge(s_fold, 2 * e + i + 1)
                    act.copy(w2[:, HI, e * EB + 2 * i:e * EB + 2 * i + 2, :].rearrange("p i h -> p (i h)"),
                             bank[MB[i]][:, :]).then_inc(s_fhi, 1)

            def gate_tanh(b):
                act.wait_ge(s_comb, 2 * (NG * b + 1))
                act.activation(tg, tg, ACT.Tanh, scale=0.5).then_inc(s_tg, 1)

            def w1_hi(g):
                i, arrived = stage_of("n", g)
                act.wait_ge(*arrived)
                act.copy(w1n[:, HI, :, COLS[g]], stage[:, i, :, 0:COUNT[g] * PART]).then_inc(s_w1hi, 1)

            steps = {"nx_hi": nx_hi, "exp": exp, "wT_copy": wT_copy, "exp_router": exp_router,
                     "pair_hi": pair_hi, "ew_copy": ew_copy, "fold_hi": fold_hi, "gate_tanh": gate_tanh,
                     "w1_hi": w1_hi}

            def prep(name, dst, i, wait=None):
                act.wait_ge(s_prep, PREP[name])
                act.copy(dst, bank[i][:, :]).then_inc(s_pa, 1)

            prep("pT1", pT[:, 1, :], 2)
            prep("kT1", kT[:, 1, :], 5)
            nx_hi(0)
            for i in range(KC):
                act.wait_ge(s_prep, PREP[f"qk{i}"])
                act.copy(qkr[:, HI, i, :, 0:NP], bank[i][:, :].rearrange("p (b n) -> p b n", b=B)).then_inc(s_pa, 1)
            prep("vT1", vT[:, 1, :], 3)
            exp(0)
            w1_hi(0)
            pair_hi(0, 0, src=0)
            pair_hi(0, 1, src=1)
            wT_copy(0)
            exp_router(0)
            w1_hi(1)
            act.wait_ge(s_gw2, 16)
            act.copy(gw2[:, HI, :, :], gw2_raw).then_inc(s_gwhi, 1)

            for s in range(SLOTS):
                b, j = divmod(s, NB)
                run_plan(steps, "act", b, j, "pre")
                if b == 0 and j == FIRST[GROUP_OF[j]]:
                    act.wait_ge(s_zb, GROUP_OF[j] + 1)
                if s == 1:
                    act.wait_ge(s_gwlo, 1)
                act.wait_ge(s_z, s + 1)
                if s >= 2:
                    act.wait_ge(s_hlo, s - 1)
                z = bank[ZB[s % 3]][:, :]
                act.activation(hf[:, s % 2, :], z, ACT.Silu, bias=zb[:, j, b:b + 1]).then_inc(s_h, 1)
                if s >= HRING:
                    h_free(act, s - HRING)
                act.activation(h[:, s % HRING, HI, :], z, ACT.Silu, bias=zb[:, j, b:b + 1]).then_inc(s_h, 1)
                run_plan(steps, "act", b, j, "post")

        @blk.vector
        def _(dve):
            chain = 0

            def link(ins):
                nonlocal chain
                chain += 1
                ins.then_inc(s_vc, 1)
                dve.wait_ge(s_vc, chain)

            def stats_of(b):
                dve.wait_ge(s_x[b % XBUFS], 16 * (b // XBUFS + 1))
                for t in range(NT):
                    ins = dve.bn_stats(stats[:, t, :], xbuf[:, b % XBUFS, t, :])
                link(ins)
                for t in range(NT):
                    ins = dve.bn_aggr(mv[:, t, :], stats[:, t, :])
                link(ins)
                if b >= 1:
                    dve.wait_ge(s_rstd, b)
                dve.tensor_scalar(ve[:, :], mv[:, :, 1], LN_EPS, None, ALU.add).then_inc(s_ve, 1)

            def normalise(b):
                dve.wait_ge(s_rstd, b + 1)
                if b >= 1:
                    dve.wait_ge(s_nhi, KC * b)
                    dve.wait_ge(s_nlo, KC * b)
                for t in range(NT):
                    ins = dve.tensor_scalar(xhat[:, t, :], xbuf[:, b % XBUFS, t, :], mv[:, t, 0:1],
                                            rstd[:, t:t + 1], ALU.subtract, ALU.mult)
                ins.then_inc(s_xhat, 1)

            def nx_full(b):
                dve.wait_ge(s_xT, b + 1)
                for k in range(KC):
                    dve.tensor_scalar(nxf[:, k, :], bank[MB[k]][:, :], cols[:, C_GAMMA + k:C_GAMMA + k + 1],
                                      cols[:, C_BETA + k:C_BETA + k + 1], ALU.mult, ALU.add).then_inc(s_nf, 1)

            def nx_lo(b):
                if b >= 2:
                    dve.wait_ge(s_z, NB * (b - 1))
                for k in range(KC):
                    dve.wait_ge(s_nhi, KC * b + k + 1)
                    dve.tensor_tensor(nx[:, b % 2, LO, k, :], nxf[:, k, :],
                                      nx[:, b % 2, HI, k, :].bitcast(F32), ALU.subtract).then_inc(s_nlo, 1)

            def over_last(v, n):
                return v.unsqueeze(2).broadcast_to([PART, NT, n])

            def score_max(b):
                dve.wait_ge(s_sc, b + 1)
                if b >= 1:
                    dve.wait_ge(s_wc, b)
                both = bank[MB[0]][:, 0:NT * SC].rearrange("p (t n) -> p t n", t=NT)
                s = both[:, :, 0:NP]
                dve.tensor_reduce(red[:, 0, :], s, AX_X, ALU.max).then_inc(s_max, 1)
                bias = lb_bc[:, b, :].unsqueeze(1).broadcast_to([PART, NT, RP])
                if b >= 1:
                    dve.wait_ge(s_lgin, b)
                dve.tensor_tensor(lgn[:, :, :], both[:, :, NP:SC], bias, ALU.add).then_inc(s_lgn, 1)
                dve.wait_ge(s_max, b + 1)
                dve.tensor_tensor(sm_d[:, :, :], s, over_last(red[:, 0, :], NP), ALU.subtract).then_inc(s_d, 1)

            def weights(b):
                dve.wait_ge(s_e, b + 1)
                link(dve.tensor_reduce(red[:, 1, :], sm_e[:, :, :], AX_X, ALU.add))
                link(dve.reciprocal(red[:, 2, :], red[:, 1, :]))
                link(dve.tensor_tensor(sm_d[:, :, :], sm_e[:, :, :], over_last(red[:, 2, :], NP), ALU.mult))
                if b >= 1:
                    dve.wait_ge(s_wt, b)
                link(dve.tensor_copy(wcat[:, :, HI, :], sm_d[:, :, :]))
                dve.tensor_tensor(wcat[:, :, LO, :], sm_d[:, :, :], wcat[:, :, HI, :].bitcast(F32),
                                  ALU.subtract).then_inc(s_wc, 1)

            def router_max(b):
                dve.wait_ge(s_lg, b + 1)
                dve.wait_ge(s_lgn, b + 1)
                src = bank[MB[1]][:, 0:NT * RP].rearrange("p (t c) -> p t c", t=NT)
                dve.tensor_tensor(lg[:, :, :], src, lgn[:, :, :], ALU.add).then_inc(s_lgin, 1)
                dve.wait_ge(s_lgin, b + 1)
                link(dve.tensor_reduce(red3[:, 0, :], lg[:, :, 0:E], AX_X, ALU.max))
                if b >= 1:
                    dve.wait_ge(s_e3, b)
                dve.tensor_tensor(lgd[:, :, 0:E], lg[:, :, 0:E], over_last(red3[:, 0, :], E),
                                  ALU.subtract).then_inc(s_d3, 1)

            def router_prob(b):
                dve.wait_ge(s_e3, b + 1)
                link(dve.tensor_reduce(red3[:, 1, :], lge[:, :, 0:E], AX_X, ALU.add))
                link(dve.reciprocal(red3[:, 2, :], red3[:, 1, :]))
                link(dve.tensor_scalar(red3[:, 3, :], red3[:, 2, :], 0.5, None, ALU.mult))
                if b >= 2:
                    dve.wait_ge(s_bs, b - 1)
                dve.tensor_tensor(ph[:, b % 2, :, 0:E], lge[:, :, 0:E], over_last(red3[:, 3, :], E),
                                  ALU.mult).then_inc(s_ph, 1)

            def pair_lo(pair, g, src=None):
                dve.wait_ge(s_phi, NG * pair + g + 1)
                src = bank[src if src is not None else PAIR_BANK[g]]
                dve.tensor_tensor(vw_pair[:, LO, COLS[g]], src[:, 0:COUNT[g] * PART],
                                  vw_pair[:, HI, COLS[g]].bitcast(F32), ALU.subtract).then_inc(s_plo, 1)

            def fold_lo(e):
                for i in range(2):
                    dve.wait_ge(s_fhi, 2 * e + i + 1)
                    blocks = slice(e * EB + 2 * i, e * EB + 2 * i + 2)
                    dve.tensor_tensor(w2[:, LO, blocks, :].rearrange("p i h -> p (i h)"), bank[MB[i]][:, :],
                                      w2[:, HI, blocks, :].rearrange("p i h -> p (i h)").bitcast(F32),
                                      ALU.subtract).then_inc(s_flo, 1)

            def w1_lo(g):
                i, _ = stage_of("n", g)
                dve.wait_ge(s_w1hi, g + 1)
                dve.tensor_tensor(w1n[:, LO, :, COLS[g]], stage[:, i, :, 0:COUNT[g] * PART],
                                  w1n[:, HI, :, COLS[g]].bitcast(F32), ALU.subtract).then_inc(s_w1lo, 1)

            def z_bias(g):
                blocks = slice(FIRST[g], FIRST[g] + COUNT[g])
                dve.wait_ge(s_zbc, g + 1)
                dve.tensor_tensor(zb[:, blocks, :],
                                  bank[ZBIAS_BANK[g]][:, 0:COUNT[g] * B].rearrange("p (j b) -> p j b", b=B),
                                  cols[:, C_B1 + FIRST[g]:C_B1 + FIRST[g] + COUNT[g]].unsqueeze(2)
                                  .broadcast_to([PART, COUNT[g], B]), ALU.add).then_inc(s_zb, 1)

            def b2_out():
                dve.wait_ge(s_bc, 32)
                dve.wait_ge(s_b2p, 1)
                dve.tensor_tensor(b2o[:, 0:2, :], bank[MB[0]][:, :].rearrange("p (e h) -> p e h", e=2),
                                  outb_bc[:, :].unsqueeze(1).broadcast_to([PART, 2, H]), ALU.add).then_inc(s_b2o, 1)
                dve.tensor_tensor(b2o[:, 2, :], bank[MB[1]][:, 0:H], outb_bc[:, :], ALU.add).then_inc(s_b2o, 1)

            steps = {"stats": stats_of, "normalise": normalise, "nx_full": nx_full, "nx_lo": nx_lo,
                     "score_max": score_max, "weights": weights, "router_max": router_max,
                     "router_prob": router_prob, "pair_lo": pair_lo, "fold_lo": fold_lo, "w1_lo": w1_lo,
                     "z_bias": z_bias, "b2_out": b2_out}

            done = 0

            def prep(name, ins):
                nonlocal done
                done += 1
                assert PV[name] == done
                ins.then_inc(s_pv, 1)

            def prep_copy(name, dst, i, n=512):
                dve.wait_ge(s_prep, PREP[name])
                prep(name, dve.tensor_copy(dst, bank[i][:, 0:n]))

            dve.memset(ones8[:, :], 1.0)
            prep_copy("cols", cols[:, :], 0, NROWS)
            dve.wait_ge(s_wr, 32)
            dve.wait_ge(s_prep, PREP["lb"])
            link(dve.memset(lb[:, :], 0.0))
            link(dve.tensor_tensor(lb[:, 0:E], bank[3][0:8, 0:E], rb_bc[:, :], ALU.add))
            dve.wait_ge(s_pool0, 2)
            prep("lb", dve.tensor_tensor(lb_diag[:, :, :], ident[0:8, 0:B].unsqueeze(2).broadcast_to([8, B, RP]),
                                         lb[:, :].unsqueeze(1).broadcast_to([8, B, RP]), ALU.mult))
            prep_copy("pT0", pT[:, 0, :], 1)
            prep_copy("wqT", wqT.rearrange("p k n -> p (k n)"), 0)
            prep_copy("lb_bc", lb_bc[:, :, :].rearrange("p b c -> p (b c)"), 3, B * RP)
            stats_of(0)
            prep_copy("kT0", kT[:, 0, :], 4)
            normalise(0)
            dve.wait_ge(s_pv, PV["cols"])
            nx_full(0)
            for i in range(KC):
                dve.wait_ge(s_pa, PA[f"qk{i}"])
                src = bank[i][:, :].rearrange("p (b n) -> p b n", b=B)
                prep(f"qk{i}", dve.tensor_tensor(qkr[:, LO, i, :, 0:NP], src, qkr[:, HI, i, :, 0:NP].bitcast(F32),
                                                 ALU.subtract))
            wr_nx = wr[:, 0:KC, :].unsqueeze(2).broadcast_to([PART, KC, B, RP])
            link(dve.tensor_copy(qkr[:, HI, :, :, NP:SC], wr_nx))
            prep("wr_lo", dve.tensor_tensor(qkr[:, LO, :, :, NP:SC], wr_nx, qkr[:, HI, :, :, NP:SC].bitcast(F32),
                                            ALU.subtract))
            nx_lo(0)
            prep_copy("vT0", vT[:, 0, :], 2)
            dve.wait_ge(s_pv, PV["lb_bc"])
            score_max(0)
            dve.wait_ge(s_prep, PREP["vwr"])
            for odd in range(2):
                src = bank[5][NP * odd:NP * (odd + 1), 0:NPAIR * RP].rearrange("p (q c) -> p q c", c=RP)
                for half in range(2):
                    dst = vwr_f[NP * half:NP * (half + 1), :, :].rearrange("p (q o) c -> p q o c", o=2)
                    ins = dve.tensor_copy(dst[:, :, odd, :], src)
            prep("vwr", ins)
            weights(0)
            dve.wait_ge(s_pv, PV["vwr"])
            link(dve.tensor_copy(vwr[:, HI, :, :], vwr_f[:, :, :]))
            prep("vwr_lo", dve.tensor_tensor(vwr[:, LO, :, :], vwr_f[:, :, :], vwr[:, HI, :, :].bitcast(F32),
                                             ALU.subtract))
            w1_lo(0)
            z_bias(0)
            pair_lo(0, 0, src=0)
            pair_lo(0, 1, src=1)
            prep("b2_bc", dve.tensor_copy(b2_bc, cols[:, C_B2:C_B2 + E * KC].unsqueeze(2)
                                          .broadcast_to([PART, E * KC, PART])))
            z_bias(1)
            router_max(0)
            router_prob(0)
            w1_lo(1)
            dve.wait_ge(s_gwhi, 1)
            dve.tensor_tensor(gw2[:, LO, :, :], gw2_raw, gw2[:, HI, :, :].bitcast(F32), ALU.subtract)\
               .then_inc(s_gwlo, 1)

            def combine(b, g):
                for half in range(2):
                    u = 2 * (NG * b + g) + half
                    dve.wait_ge(s_acc, u + 1)
                    src = bank[AB[u % 3]][:, :].rearrange("p (i h) -> p i h", i=2)
                    tiles = slice(2 * half, 2 * half + 2)
                    if g == 0:
                        if b >= 1:
                            dve.wait_ge(s_y, b)
                        dve.tensor_tensor(tg[:, tiles, :], src, gb2_bc[:, :].unsqueeze(1)
                                          .broadcast_to([PART, 2, H]), ALU.add).then_inc(s_comb, 1)
                        continue
                    if g == 1 and half == 0:
                        dve.wait_ge(s_bs, b + 1)
                        if b >= 1:
                            dve.wait_ge(s_o, b)
                    if g > 1:
                        dve.wait_ge(s_comb, u - 1)
                    for i in range(2):
                        t = 2 * half + i
                        ins = dve.scalar_tensor_tensor(acc[:, t, :], src[:, i, :], ph[:, b % 2, t, g - 1:g],
                                                       (bsum if g == 1 else acc)[:, t, :], ALU.mult, ALU.add)
                    ins.then_inc(s_comb, 1)

            def gated(b):
                dve.wait_ge(s_tg, b + 1)
                dve.wait_ge(s_comb, 2 * NG * (b + 1))
                dve.scalar_tensor_tensor(acc, tg, 1.0, acc, ALU.add, ALU.mult).then_inc(s_y, 1)

            for s in range(SLOTS + LAG):
                b, j = divmod(s, NB)
                if s < SLOTS:
                    run_plan(steps, "dve", b, j, "pre")
                    dve.wait_ge(s_h, 2 * (s + 1))
                    if s >= HRING:
                        h_free(dve, s - HRING)
                    dve.tensor_tensor(h[:, s % HRING, LO, :], hf[:, s % 2, :],
                                      h[:, s % HRING, HI, :].bitcast(F32), ALU.subtract).then_inc(s_hlo, 1)
                if s >= LAG:
                    b2, j2 = divmod(s - LAG, NB)
                    g = GROUP_OF[j2]
                    if j2 == FIRST[g] + COUNT[g] - 1:
                        combine(b2, g)
                        if g == NG - 1:
                            gated(b2)
                if s < SLOTS:
                    run_plan(steps, "dve", b, j, "post")

        @blk.gpsimd
        def _(pool):
            chain = 0

            def link(ins):
                nonlocal chain
                chain += 1
                ins.then_inc(s_gc, 1)
                pool.wait_ge(s_gc, chain)

            def reciprocal_std(b):
                pool.wait_ge(s_ve, b + 1)
                if b >= 1:
                    pool.wait_ge(s_xhat, b)
                pool.tensor_tensor(rstd[:, :], ve[:, :], minus_half[:, :], ALU.pow).then_inc(s_rstd, 1)

            def bias_sum(b):
                pool.wait_ge(s_ph, b + 1)
                pool.wait_ge(s_b2o, 2)
                if b >= 1:
                    pool.wait_ge(s_comb, 2 * (NG * (b - 1) + 2))
                for t in range(NT):
                    p = ph[:, b % 2, t, :]
                    pool.tensor_scalar(bsum[:, t, :], b2o[:, 0, :], p[:, 0:1], 0.0, ALU.mult, ALU.add)
                    for e in (1, 2):
                        ins = pool.tensor_scalar(btmp[:, e - 1, :], b2o[:, e, :], p[:, e:e + 1], 0.0,
                                                 ALU.mult, ALU.add)
                    link(ins)
                    link(pool.tensor_tensor(bsum[:, t, :], bsum[:, t, :], btmp[:, 0, :], ALU.add))
                    ins = pool.tensor_tensor(bsum[:, t, :], bsum[:, t, :], btmp[:, 1, :], ALU.add)
                    if t < NT - 1:
                        link(ins)
                ins.then_inc(s_bs, 1)

            pool.memset(minus_half[:, :], -0.5)
            pool.memset(ident[:, :], 0.0).then_inc(s_pool0, 1)
            pool.wait_ge(s_pool0, 1)
            pool.affine_select(out=ident[:, :], in_=ident[:, :], compare_op=ALU.not_equal, fill=1.0, base=0,
                               pattern=[[-1, PART]], channel_multiplier=1).then_inc(s_pool0, 1)
            pool.memset(wr[:, :, :], 0.0).then_inc(s_pool0, 1)
            pool.wait_ge(s_pool0, 2)
            pool.tensor_copy(ident_r[:, :], ident[:, :]).then_inc(s_pool0, 1)
            reciprocal_std(0)
            reciprocal_std(1)
            bias_sum(0)
            for b in range(B):
                if b >= 1:
                    pool.wait_ge(s_y, b)
                    pool.tensor_tensor(xbuf[:, (b - 1) % XBUFS, :, :], xbuf[:, (b - 1) % XBUFS, :, :], acc,
                                       ALU.add).then_inc(s_o, 1)
                if b + 2 < B:
                    reciprocal_std(b + 2)
                if b + 1 < B:
                    bias_sum(b + 1)
            pool.wait_ge(s_y, B)
            pool.tensor_tensor(xbuf[:, (B - 1) % XBUFS, :, :], xbuf[:, (B - 1) % XBUFS, :, :], acc,
                               ALU.add).then_inc(s_o, 1)


_INS = ["x", "cond_1024", "ctx_1024", "L0_xcond_ln_gamma", "L0_xcond_ln_beta", "L0_xcond_Wq", "L0_xcond_Wk",
        "L0_xcond_Wv", "L0_xcond_router_W", "L0_xcond_router_b", "L0_xcond_e_w1", "L0_xcond_e_b1",
        "L0_xcond_e_w2", "L0_xcond_e_b2", "L0_xcond_gate_w1", "L0_xcond_gate_b1", "L0_xcond_gate_w2",
        "L0_xcond_gate_b2", "L0_xcond_out_w", "L0_xcond_out_b"]


def kernel(**inputs):
    import numpy as _np
    import concourse.bacc as _bacc
    from concourse import mybir as _mybir
    from concourse.bass_utils import run_bass_kernel_spmd as _run

    nc = _bacc.Bacc("TRN2", target_bir_lowering=False, num_devices=1)
    arrays, args = {}, []
    for name in _INS:
        a = _np.ascontiguousarray(inputs[name])
        arrays[f"in_{name}_dram"] = a
        args.append(nc.dram_tensor(f"in_{name}_dram", a.shape, _mybir.dt.from_np(a.dtype), kind="ExternalInput").ap())
    shape = tuple(inputs["x"].shape)
    args.append(nc.dram_tensor("out_0_dram", shape, _mybir.dt.float32, kind="ExternalOutput").ap())
    build(nc, *args)
    r = _run(nc, [arrays], core_ids=[0])
    return r.results[0]["out_0_dram"]
```

```python
from contextlib import ExitStack

import concourse.bass as bass
from concourse import mybir

F32 = mybir.dt.float32
F32R = mybir.dt.float32r
ALU = mybir.AluOpType
ACT = mybir.ActivationFunctionType
AX_X = mybir.AxisListType.X

PART = 128
LN_EPS = 1e-05
SPLIT_PASSES = ((0, 0), (0, 1), (1, 0))
HI, LO = 0, 1


def build(nc, x, cond, ctx, ln_gamma, ln_beta, Wq, Wk, Wv, router_W, router_b,
          e_w1, e_b1, e_w2, e_b2, gate_w1, gate_b1, gate_w2, gate_b2, out_w, out_b, out):
    B, T, H = x.shape
    NP = ctx.shape[1]
    E, _, R = e_w1.shape
    KC = H // PART
    NT = T // PART
    GB = H // PART
    EB = R // PART
    NB = GB + E * EB
    NCOL = NB * PART
    RP = 4
    assert 2 * NP == PART and B * NP == 512 and T == 512 and KC == 2
    FIRST = [0] + [GB + EB * e for e in range(E)]
    COUNT = [GB] + [EB] * E
    COLS = [slice(f * PART, (f + n) * PART) for f, n in zip(FIRST, COUNT)]
    NG = 1 + E
    GROUP_OF = [g for g in range(NG) for _ in range(COUNT[g])]
    STATS_SLOT = 8
    LAG = 2
    SLOTS = B * NB
    EARLY = 2

    es = ExitStack()
    with es:
        def sb(name, shape, dt=F32):
            return es.enter_context(nc.sbuf_tensor(name, shape, dt))

        def sem(name):
            return es.enter_context(nc.semaphore(name))

        XBUFS = 3
        xbuf = sb("xbuf", [PART, XBUFS, NT, H])
        w1n = sb("w1n", [PART, 2, KC, NCOL], F32R)
        VCOL = RP + NCOL
        VCOLS = [slice(RP + c.start if g else 0, RP + c.stop) for g, c in enumerate(COLS)]
        vw_pair = sb("vw_pair", [PART, 2, VCOL], F32R)
        vw = sb("vw", [PART, 2, VCOL], F32R)
        w2 = sb("w2", [PART, 2, E * EB, H], F32R)
        gw2 = sb("gw2", [PART, 2, GB, H], F32R)
        SC = NP + RP
        qkr = sb("qkr", [PART, 2, KC, B, SC], F32R)
        HRING = 3
        h = sb("h", [PART, HRING, 2, T], F32R)
        hf = sb("hf", [PART, 2, T])
        nx = sb("nx", [PART, 2, 2, KC, T], F32R)
        xw = sb("xw", [PART, NT * H])
        xhat = xw[:, :].rearrange("p (t h) -> p t h", t=NT)
        nxf = xw[:, :].rearrange("p (k t) -> p k t", k=KC)
        sm_d = sb("sm_d", [PART, NT, SC])
        sm_e = sb("sm_e", [PART, NT, SC])
        wcat = sb("wcat", [PART, NT, 2, NP], F32R)
        wT = sb("wT", [PART, 2, T], F32R)
        b2o = sb("b2o", [PART, E, H])
        outb_bc = sb("outb_bc", [PART, H])
        gb2_bc = sb("gb2_bc", [PART, H])
        ident = sb("ident", [PART, PART])
        ident_r = sb("ident_r", [PART, PART], F32R)
        ones8 = sb("ones8", [8, PART])
        NROWS = NB + 2 * KC + E * KC + B * KC
        rows = hf[0:NROWS, 0, 0:PART]
        gw2_raw = hf[:, 1, :].rearrange("p (k n) -> p k n", k=GB)
        cols = sb("cols", [PART, NROWS])
        C_B1, C_GAMMA, C_BETA = 0, NB, NB + KC
        C_B2 = C_BETA + KC
        C_COND = C_B2 + E * KC
        zb = sb("zb", [PART, NB, B])
        wr = sb("wr", [PART, 3 * KC, RP])
        rb_bc = sb("rb_bc", [8, E])
        lb = sb("lb", [8, RP])
        lb_diag = sb("lb_diag", [8, B, RP])
        lb_bc = sb("lb_bc", [PART, B, RP])
        stats = sb("stats", [PART, NT, 6])
        mv = sb("mv", [PART, NT, 2])
        ve = sb("ve", [PART, NT])
        rstd = sb("rstd", [PART, NT])
        minus_half = sb("minus_half", [PART, NT])
        red = sb("red", [PART, 3, NT])
        red3 = sb("red3", [PART, 4, NT])
        lgn = sb("lgn", [PART, NT, RP])
        lg = sb("lg", [PART, NT, RP])
        lgd = sb("lgd", [PART, NT, RP])
        lge = sb("lge", [PART, NT, RP])
        ph = sb("ph", [PART, 2, NT, RP])
        raw = ExitStack()
        w1v = raw.enter_context(nc.sbuf_tensor("w1v", [PART, KC, VCOL], F32))
        vT = raw.enter_context(nc.sbuf_tensor("vT", [PART, KC, B * NP], F32))
        STAGES = 3
        stage = raw.enter_context(nc.sbuf_tensor("stage", [PART, STAGES, KC, 512], F32))
        work = raw.enter_context(nc.sbuf_tensor("work", [PART, 5120], F32))
        ctx_raw = work[:, 0:1024].rearrange("p (t h) -> p t h", t=4)
        pT = work[:, 1024:2048].rearrange("p (k n) -> p k n", k=KC)
        wkT = work[:, 2048:2560].rearrange("p (k n) -> p k n", k=KC)
        gT = work[:, 2560:3072].rearrange("p (k n) -> p k n", k=KC)
        wv_raw = work[:, 3072:3584].rearrange("p (k n) -> p k n", k=KC)
        wq_raw = work[:, 3584:4096].rearrange("p (k n) -> p k n", k=KC)
        wk_raw = work[:, 4096:4608].rearrange("p (k n) -> p k n", k=KC)
        wqT = work[:, 4608:5120].rearrange("p (k n) -> p k n", k=KC)
        acc = work[:, 0:1024].rearrange("p (t h) -> p t h", t=NT)
        tg = work[:, 1024:2048].rearrange("p (t h) -> p t h", t=NT)
        bsum = work[:, 2048:3072].rearrange("p (t h) -> p t h", t=NT)
        btmp = work[:, 3072:3584].rearrange("p (i h) -> p i h", i=2)
        ow_raw = work[:, 3584:4096].rearrange("p (k n) -> p k n", k=KC)
        b2_bc = work[:, 4096:4096 + E * KC * PART].rearrange("p (c n) -> p c n", n=PART)
        ewT = work[:, 4096:5120].rearrange("p (k n) -> p k n", k=KC)

        raw.close()
        w1v_lo = sb("w1v_lo", [PART, KC, VCOL], F32R)
        vT_lo = sb("vT_lo", [PART, KC, B * NP], F32R)
        HI_STAGE = (None, 2, 0, 1)
        stage_hi = sb("stage_hi", [PART, STAGES, KC, 512], F32R)
        SLOT_WORK = 3584
        sb("slot_work", [PART, SLOT_WORK])
        work_hi = sb("work_hi", [PART, 5120 - SLOT_WORK], F32R)
        VGATE = VCOLS[0].stop
        w1v_hi = [work_hi[:, 0:KC * VGATE].rearrange("p (k n) -> p k n", k=KC)] \
            + [stage_hi[:, i, :, :] for i in HI_STAGE[1:]]
        vT_hi = work_hi[:, KC * VGATE:KC * VGATE + KC * (B * NP - PART)] \
            .rearrange("p (k n) -> p k n", k=KC)
        VSPLITS = ("w1v1", "w1v2", "w1v3", "w1v0", "vT")
        VSPLIT = {n: i + 1 for i, n in enumerate(VSPLITS)}

        bank = [es.enter_context(nc.psum_tensor(f"bank{i}", [PART, 512], F32)) for i in range(8)]
        PAIR_BANK = (7, 6, 7, 6)
        FIRST_PAIR_BANK = (3, 4)
        B2_BANK = (6, 5)
        ZBIAS_BANK = (2, 5, 6, 7)
        ZB, AB, MB = (0, 1, 2), (3, 4, 5), (6, 7)

        s_x = [sem(f"s_x{i}") for i in range(XBUFS)]
        s_rows, s_ctx, s_wk, s_wq, s_wv = (sem(n) for n in ("s_rows", "s_ctx", "s_wk", "s_wq", "s_wv"))
        s_wr, s_bc, s_ow, s_gw2 = (sem(n) for n in ("s_wr", "s_bc", "s_ow", "s_gw2"))
        s_w1v = [sem(f"s_w1v{c}") for c in range(NG)]
        s_stage = [sem(f"s_stage{i}") for i in range(STAGES)]
        s_dup = [sem(f"s_dup{c}") for c in range(NG)]
        s_out = sem("s_out")
        s_pool0 = sem("s_pool0")
        s_prep = sem("s_prep")
        s_pv = sem("s_pv")
        s_pa = sem("s_pa")
        s_w1hi, s_w1lo = sem("s_w1hi"), sem("s_w1lo")
        s_gwhi, s_gwlo = sem("s_gwhi"), sem("s_gwlo")
        s_zbc = sem("s_zbc")
        s_zb = sem("s_zb")
        s_b2p, s_b2o = sem("s_b2p"), sem("s_b2o")
        s_vwp, s_phi, s_plo = sem("s_vwp"), sem("s_phi"), sem("s_plo")
        s_vhi, s_vlo = sem("s_vhi"), sem("s_vlo")
        s_ewT, s_ewc = sem("s_ewT"), sem("s_ewc")
        s_fold, s_fhi, s_flo = sem("s_fold"), sem("s_fhi"), sem("s_flo")
        s_ve, s_rstd, s_xhat = sem("s_ve"), sem("s_rstd"), sem("s_xhat")
        s_xT, s_nf, s_nhi, s_nlo = sem("s_xT"), sem("s_nf"), sem("s_nhi"), sem("s_nlo")
        s_sc, s_d, s_e, s_wc, s_wt, s_wT = (sem(n) for n in ("s_sc", "s_d", "s_e", "s_wc", "s_wt", "s_wT"))
        s_lg, s_lgin, s_d3, s_e3, s_ph = (sem(n) for n in ("s_lg", "s_lgin", "s_d3", "s_e3", "s_ph"))
        s_cross, s_s = sem("s_cross"), sem("s_s")
        s_max, s_lgn = sem("s_max"), sem("s_lgn")
        s_z = sem("s_z")
        s_h = sem("s_h")
        s_hlo = sem("s_hlo")
        s_w2 = sem("s_w2")
        s_acc = sem("s_acc")
        s_comb = sem("s_comb")
        s_tg = sem("s_tg")
        s_bs = sem("s_bs")
        s_y = sem("s_y")
        s_o = sem("s_o")
        s_vc, s_gc = sem("s_vc"), sem("s_gc")

        blk = es.enter_context(nc.Block())

        staged = [("n", 0), ("c", 0), ("n", 1), ("c", 1), ("w2", 0), ("n", 2), ("c", 2), ("w2", 1),
                  ("n", 3), ("c", 3), ("w2", 2)]
        assert NG == 4

        def stage_of(kind, g):
            u = staged.index((kind, g))
            return u % STAGES, (s_stage[u % STAGES], 16 * (u // STAGES + 1))

        FIRST_PLAN = {1: ["zb1"], 2: ["ewT0", "split2"], 3: ["fold0"], 4: ["vwp2", "zb2"], 5: ["ewT1"],
                      6: ["xT", "split3"], 7: ["fold1"], 8: ["vwp3", "zb3", "vsplit1"], 9: ["ewT2", "vsplit2"],
                      10: ["sc"], 11: ["fold2"], 12: ["wt", "vsplit3", "vsplit0"], 13: ["lg", "vsplit4"]}
        EVEN_PLAN = {1: ["xT"], 5: ["sc"], 8: ["wt"], 10: ["lg"]}
        ODD_PLAN = {1: ["xT"], 2: ["vwp0"], 3: ["vwp1"], 5: ["sc"], 7: ["vwp2"], 8: ["wt"], 10: ["lg"], 11: ["vwp3"]}

        def plan(engine, b, j, when):
            nxt = b + 1
            at = FIRST_PLAN if b == 0 else ODD_PLAN if b % 2 == 1 else EVEN_PLAN
            steps = []
            for now in at.get(j, ()) if nxt < B else ():
                name = now.rstrip("0123456789")
                n = int(now[len(name):] or 0)
                args, pre, post = {
                    "xT": ((nxt,), {"act": ["nx_hi"], "dve": ["nx_full", "nx_lo"]}, {}),
                    "sc": ((nxt,), {"act": ["exp"], "dve": ["score_max"]}, {"dve": ["weights"]}),
                    "wt": ((nxt,), {"act": ["wT_copy"]}, {}),
                    "lg": ((nxt,), {"act": ["exp_router"], "dve": ["router_max"]}, {"dve": ["router_prob"]}),
                    "vwp": (((b + 1) // 2, n), {"act": ["pair_hi"], "dve": ["pair_lo"]}, {}),
                    "ewT": ((n,), {"act": ["ew_copy"]}, {}),
                    "fold": ((n,), {"act": ["fold_hi"], "dve": ["fold_lo"]}, {}),
                    "zb": ((n,), {"dve": ["z_bias"]}, {}),
                    "split": ((n,), {}, {"act": ["w1_hi"], "dve": ["w1_lo"]}),
                    "vsplit": ((n,), {}, {"act": ["v_hi"], "dve": ["v_lo"]}),
                }[name]
                if engine == "pe":
                    steps += [(name, *args)] if when == "pre" and "split" not in name else []
                else:
                    steps += [(f, *args) for f in (pre if when == "pre" else post).get(engine, [])]
            if when == "post" and engine == "act" and j == GB + LAG:
                steps.append(("gate_tanh", b))
            if when == "post" and engine == "dve":
                if b == 0 and j in (1, 2):
                    steps.append(("stats" if j == 1 else "normalise", 1))
                if b + 2 < B and j in (STATS_SLOT, STATS_SLOT + 2):
                    steps.append(("stats" if j == STATS_SLOT else "normalise", b + 2))
            return steps

        def run_plan(steps, engine, b, j, when):
            for name, *args in plan(engine, b, j, when):
                steps[name](*args)

        PREP = {n: i + 1 for i, n in enumerate(
            ("wkT", "wqT", "pT0", "pT1", "gT", "vT0", "vT1", "cols", "qk0", "qk1", "lb", "lb_bc"))}
        PV = {n: i + 1 for i, n in enumerate(
            ("wkT", "wqT", "pT0", "gT", "cols", "lb", "qk0", "qk1", "lb_bc"))}
        PA = {n: i + 1 for i, n in enumerate(("pT1", "vT0", "vT1", "qk0", "qk1"))}

        def score_parts(half):
            return bank[MB[half]][:, 0:4 * SC].rearrange("p (t a n) -> p t a n", t=2, a=2)

        small = {"gate_b1": (C_B1, gate_b1.rearrange("(r c) -> r c", c=PART)),
                 "e_b1": (C_B1 + GB, e_b1.rearrange("e (i c) -> (e i) c", c=PART)),
                 "gamma": (C_GAMMA, ln_gamma.rearrange("(r c) -> r c", c=PART)),
                 "beta": (C_BETA, ln_beta.rearrange("(r c) -> r c", c=PART)),
                 "e_b2": (C_B2, e_b2.rearrange("e (i c) -> (e i) c", c=PART)),
                 "cond": (C_COND, cond.rearrange("b (i c) -> (b i) c", c=PART))}

        def load_rows(eng, name):
            first, src = small[name]
            eng.dma_start(rows[first:first + src.shape[0], :], src).then_inc(s_rows, 16)

        @blk.sync
        def _(sp):
            def load_x(b):
                sp.dma_start(xbuf[:, b % XBUFS, :, :], x[b].rearrange("(t p) h -> p t h", p=PART))\
                  .then_inc(s_x[b % XBUFS], 16)

            def first_layer(g, part):
                w = gate_w1 if g == 0 else e_w1[g - 1]
                return w[part * H:(part + 1) * H, :].rearrange("(k p) n -> p k n", p=PART)

            def load_w1v(g):
                sp.dma_start(w1v[:, :, RP + COLS[g].start:RP + COLS[g].stop], first_layer(g, 1)).then_inc(s_w1v[g], 16)

            def load_staged(kind, g):
                u = staged.index((kind, g))
                if u >= STAGES:
                    before, bg = staged[u - STAGES]
                    if before == "n":
                        sp.wait_ge(s_w1lo, bg + 1)
                    elif before == "c":
                        sp.wait_ge(s_zbc, bg + 1)
                    else:
                        sp.wait_ge(s_ewT, bg + 1)
                if kind == "w2":
                    dst = stage[:, u % STAGES, :, :].rearrange("p k n -> p (k n)").rearrange(
                        "p (i h) -> p i h", h=H)
                    src = e_w2[g].rearrange("(i p) h -> p i h", p=PART)
                else:
                    dst = stage[:, u % STAGES, :, 0:COUNT[g] * PART]
                    src = first_layer(g, 0 if kind == "n" else 2)
                sp.dma_start(dst, src).then_inc(s_stage[u % STAGES], 16)

            def square(w):
                return w.rearrange("(k p) n -> p k n", p=PART)

            def load_vw(b, g):
                sp.wait_ge(s_plo, NG * (b // 2) + g + 1)
                sp.wait_ge(s_phi, NG * (b // 2) + g + 1)
                if b >= 1:
                    sp.wait_ge(s_z, NB * (b - 1) + FIRST[g] + COUNT[g])
                r = NP * (b % 2)
                for half in range(2):
                    sp.dma_start(vw[NP * half:NP * (half + 1), :, VCOLS[g]].bitcast(F32),
                                 vw_pair[r:r + NP, :, VCOLS[g]].bitcast(F32)).then_inc(s_dup[g], 16)

            sp.dma_start(wk_raw, square(Wk)).then_inc(s_wk, 16)
            sp.dma_start(wq_raw, square(Wq)).then_inc(s_wq, 16)
            sp.dma_start(ctx_raw, ctx.rearrange("b q h -> (b q) h").rearrange("(t p) h -> p t h", p=PART))\
              .then_inc(s_ctx, 16)
            load_x(0)
            sp.dma_start(wv_raw, square(Wv)).then_inc(s_wv, 16)
            load_staged("n", 0)
            load_w1v(0)
            load_staged("c", 0)
            load_w1v(1)
            load_staged("n", 1)
            sp.wait_ge(s_prep, PREP["wqT"])
            sp.dma_start(ow_raw, square(out_w)).then_inc(s_ow, 16)
            load_x(1)
            load_staged("c", 1)
            load_vw(0, 0)
            load_w1v(2)
            load_vw(0, 1)
            load_staged("w2", 0)
            load_staged("n", 2)
            load_w1v(3)
            load_staged("c", 2)
            load_x(2)
            load_staged("w2", 1)
            load_staged("n", 3)
            load_vw(0, 2)
            load_staged("c", 3)
            load_staged("w2", 2)
            load_vw(0, 3)

            def store(b):
                for half in range(2):
                    sp.wait_ge(s_o, 2 * b + half + 1)
                    tiles = slice(2 * half, 2 * half + 2)
                    sp.dma_start(out[b].rearrange("(t p) h -> p t h", p=PART)[:, tiles, :],
                                 xbuf[:, b % XBUFS, tiles, :]).then_inc(s_out, 16)

            for b in range(B):
                for g in range(NG):
                    if b + 1 < B:
                        load_vw(b + 1, g)
                    if g == 0 and b >= 1:
                        store(b - 1)
                        if b + 2 < B:
                            sp.wait_ge(s_out, 32 * b)
                            load_x(b + 2)
            store(B - 1)
            sp.wait_ge(s_out, 32 * B)

        @blk.tensor
        def _(pe):
            readers = {}

            def take(i, last_reader=None):
                if i in readers:
                    pe.wait_ge(*readers[i])
                readers[i] = last_reader
                return bank[i]

            def split_product(dst, pairs, first=True, last=True):
                n = len(pairs) * len(SPLIT_PASSES)
                i = 0
                for lhs, rhs in pairs:
                    for a, c in SPLIT_PASSES:
                        mm = pe.matmul(dst, lhs(a), rhs(c), start=first and i == 0, stop=last and i == n - 1)
                        i += 1
                return mm

            def x_transpose(b):
                pe.wait_ge(s_xhat, b + 1)
                for k in range(KC):
                    dst = take(MB[k], (s_nf, KC * b + k + 1))
                    for t in range(NT):
                        mm = pe.transpose(dst[:, t * PART:(t + 1) * PART], xhat[:, t, k * PART:(k + 1) * PART],
                                          ident[:, :])
                mm.then_inc(s_xT, 1)

            def nx_lhs(b, k, t):
                return lambda part: nx[:, b % 2, part, k, t * PART:(t + 1) * PART]

            def scores(b):
                pe.wait_ge(s_nlo, KC * (b + 1))
                pe.wait_ge(s_nhi, KC * (b + 1))
                for t in range(NT):
                    if t % 2 == 0:
                        dst = take(MB[t // 2], (s_s, 2 * b + t // 2 + 1))
                    o = dst[:, (t % 2) * 2 * SC:(t % 2 + 1) * 2 * SC]
                    for k in range(KC):
                        pe.matmul(o, nx_lhs(b, k, t)(HI), qkr[:, :, k, b, :], start=k == 0, stop=False,
                                  skip_group_check=True)
                        mm = pe.matmul(o[:, 0:SC], nx_lhs(b, k, t)(LO), qkr[:, HI, k, b, :], start=False,
                                       stop=k == KC - 1, skip_group_check=True)
                mm.then_inc(s_sc, 1)

            def w_transpose(b):
                pe.wait_ge(s_wc, b + 1)
                if b == 0:
                    pe.wait_ge(s_pool0, 4)
                dst = take(MB[1], (s_wT, b + 1))
                for t in range(NT):
                    mm = pe.transpose(dst[:, t * PART:(t + 1) * PART].bitcast(F32R),
                                      wcat[:, t, :, :].rearrange("p a n -> p (a n)"), ident_r[:, :])
                mm.then_inc(s_wt, 1)

            def logits(b):
                pe.wait_ge(s_wT, b + 1)
                pe.wait_ge(s_dup[0], 32 * (b + 1))
                dst = take(MB[1], (s_lgin, b + 1))
                for t in range(NT):
                    mm = pe.matmul(dst[:, 2 * t * RP:2 * (t + 1) * RP], wT[:, b % 2, t * PART:(t + 1) * PART],
                                   vw[:, :, 0:RP], start=True, stop=True)
                mm.then_inc(s_lg, 1)

            def pair_product(pair, g, dst=None):
                pe.wait_ge(s_w1v[g], 16)
                done = (s_plo, NG * pair + g + 1)
                dst = take(dst if dst is not None else PAIR_BANK[g], done)
                if g == 0 and pair == 0:
                    pe.wait_ge(s_pool0, 5)
                n = VCOLS[g].stop - VCOLS[g].start
                if pair == 0:
                    for k in range(KC):
                        mm = pe.matmul(dst[:, 0:n], vT[:, k, 0:PART], w1v[:, k, VCOLS[g]],
                                       start=k == 0, stop=k == KC - 1)
                else:
                    if pair == 1:
                        ready = max(VSPLIT[f"w1v{g}"], VSPLIT["vT"])
                        pe.wait_ge(s_vhi, ready)
                        pe.wait_ge(s_vlo, ready)
                    first = (pair - 1) * PART
                    v = (vT_hi[:, :, first:first + PART], vT_lo[:, :, PART + first:2 * PART + first])
                    w = (w1v_hi[g], w1v_lo[:, :, VCOLS[g]])
                    mm = split_product(dst[:, 0:n], [(lambda part, k=k: v[part][:, k, :],
                                                      lambda part, k=k: w[part][:, k, :]) for k in range(KC)])
                mm.then_inc(s_vwp, 1)

            def w2_transpose(e):
                i, arrived = stage_of("w2", e)
                pe.wait_ge(*arrived)
                raw = stage[:, i, :, :].rearrange("p k n -> p (k n)").rearrange("p (i h) -> p i h", h=H)
                for k in range(KC):
                    dst = take(MB[k], (s_ewc, KC * e + k + 1))
                    for i in range(EB):
                        mm = pe.transpose(dst[:, i * PART:(i + 1) * PART], raw[:, i, k * PART:(k + 1) * PART],
                                          ident[:, :])
                mm.then_inc(s_ewT, 1)

            def w2_fold(e):
                pe.wait_ge(s_ewc, KC * (e + 1))
                pe.wait_ge(s_ow, 16)
                for i in range(EB):
                    if i % 2 == 0:
                        dst = take(MB[i // 2], (s_flo, 2 * e + i // 2 + 1))
                    for k in range(KC):
                        mm = pe.matmul(dst[:, (i % 2) * H:(i % 2 + 1) * H], ewT[:, k, i * PART:(i + 1) * PART],
                                       ow_raw[:, k, :], start=k == 0, stop=k == KC - 1)
                    if i % 2 == 1:
                        mm.then_inc(s_fold, 1)

            def anchor_product(g):
                i, arrived = stage_of("c", g)
                pe.wait_ge(*arrived)
                dst = take(ZBIAS_BANK[g], (s_zb, g + 1))
                for c in range(COUNT[g]):
                    for k in range(KC):
                        mm = pe.matmul(dst[:, c * B:(c + 1) * B], stage[:, i, k, c * PART:(c + 1) * PART],
                                       cols[:, C_COND + k:C_COND + B * KC:KC], start=k == 0, stop=k == KC - 1)
                mm.then_inc(s_zbc, 1)

            def b2_product():
                pe.wait_ge(s_ow, 16)
                pe.wait_ge(s_pool0, 8)
                for e in range(E):
                    if e % 2 == 0:
                        dst = take(B2_BANK[e // 2], (s_b2o, e // 2 + 1))
                    for k in range(KC):
                        mm = pe.matmul(dst[:, (e % 2) * H:(e % 2 + 1) * H], b2_bc[:, e * KC + k, :],
                                       ow_raw[:, k, :], start=k == 0, stop=k == KC - 1)
                mm.then_inc(s_b2p, 1)

            steps = {"xT": x_transpose, "sc": scores, "wt": w_transpose, "lg": logits, "vwp": pair_product,
                     "ewT": w2_transpose, "fold": w2_fold, "zb": anchor_product}

            done = 0

            def prep(name, mm):
                nonlocal done
                done += 1
                assert PREP[name] == done
                mm.then_inc(s_prep, 1)

            def product(name, i, reader, lhs, rhs, n=B * NP, m=PART):
                dst = take(i, reader)
                for k in range(KC):
                    mm = pe.matmul(dst[0:m, 0:n], lhs(k), rhs(k), start=k == 0, stop=k == KC - 1)
                prep(name, mm)

            def turn(name, i, reader, raw):
                dst = take(i, reader)
                for j in range(KC):
                    for k in range(KC):
                        mm = pe.transpose(dst[:, j * H + k * PART:j * H + (k + 1) * PART],
                                          raw[:, k, j * PART:(j + 1) * PART], ident[:, :])
                prep(name, mm)

            pe.wait_ge(s_pool0, 2)
            pe.wait_ge(s_wk, 16)
            turn("wkT", 0, (s_pv, PV["wkT"]), wk_raw)
            pe.wait_ge(s_wq, 16)
            turn("wqT", 1, (s_pv, PV["wqT"]), wq_raw)
            pe.wait_ge(s_ctx, 16)
            for k in range(KC):
                dst = take(2 + k, (s_pv, PV["pT0"]) if k == 0 else (s_pa, PA["pT1"]))
                for t in range(4):
                    mm = pe.transpose(dst[:, t * PART:(t + 1) * PART], ctx_raw[:, t, k * PART:(k + 1) * PART],
                                      ident[:, :])
                prep(f"pT{k}", mm)
            pe.wait_ge(s_pv, PV["wqT"])
            dst = take(4, (s_pv, PV["gT"]))
            for j in range(KC):
                for k in range(KC):
                    mm = pe.matmul(dst[:, j * H:(j + 1) * H], wkT[:, k, j * PART:(j + 1) * PART], wqT[:, k, :],
                                   start=k == 0, stop=k == KC - 1)
            prep("gT", mm)

            def values(j):
                product(f"vT{j}", 2 + j, (s_pa, PA[f"vT{j}"]), lambda k: wv_raw[:, k, j * PART:(j + 1) * PART],
                        lambda k: pT[:, k, :])

            pe.wait_ge(s_wv, 16)
            pe.wait_ge(s_pv, PV["pT0"])
            pe.wait_ge(s_pa, PA["pT1"])
            values(0)
            values(1)
            pe.wait_ge(s_rows, 96)
            prep("cols", pe.transpose(take(5, (s_pv, PV["cols"]))[:, 0:NROWS], rows,
                                      ident[0:NROWS, 0:NROWS]))
            x_transpose(0)
            pe.wait_ge(s_pv, PV["gT"])
            for i in range(KC):
                product(f"qk{i}", i, (s_pv, PV[f"qk{i}"]),
                        lambda j: gT[:, j, i * PART:(i + 1) * PART], lambda j: pT[:, j, :])
            pe.wait_ge(s_wr, 32)
            pe.wait_ge(s_pv, PV["cols"])
            product("lb", 5, (s_pv, PV["lb"]), lambda k: cols[:, C_COND + k:C_COND + B * KC:KC],
                    lambda k: wr[:, 2 * KC + k, :], n=RP, m=B)
            pe.wait_ge(s_pa, PA["vT1"])
            pair_product(0, 0, dst=FIRST_PAIR_BANK[0])
            pe.wait_ge(s_pv, PV["lb"])
            prep("lb_bc", pe.matmul(take(5, (s_pv, PV["lb_bc"]))[:, 0:B * RP], ones8[:, :],
                                    lb_diag[:, :, :].rearrange("p b c -> p (b c)"), start=True, stop=True))
            pair_product(0, 1, dst=FIRST_PAIR_BANK[1])
            pe.wait_ge(s_pv, PV["qk1"])
            pe.wait_ge(s_pool0, 7)
            scores(0)
            anchor_product(0)

            def first_layer_nx(s):
                b, j = divmod(s, NB)
                g = GROUP_OF[j]
                if b == 0 and j == FIRST[g]:
                    pe.wait_ge(s_w1hi, g + 1)
                    pe.wait_ge(s_w1lo, g + 1)
                if j == 0:
                    pe.wait_ge(s_nlo, KC * (b + 1))
                    pe.wait_ge(s_nhi, KC * (b + 1))
                dst = (bank[ZB[s % 3]] if s >= 3 else take(ZB[s % 3]))[:, :]
                block = slice(j * PART, (j + 1) * PART)
                split_product(dst, [(lambda part, k=k: w1n[:, part, k, block],
                                     lambda part, k=k: nx[:, b % 2, part, k, :]) for k in range(KC)], last=False)

            def first_layer_evidence(s):
                b, j = divmod(s, NB)
                g = GROUP_OF[j]
                if j == 0:
                    pe.wait_ge(s_wT, b + 1)
                if j == FIRST[g]:
                    pe.wait_ge(s_dup[g], 32 * (b + 1))
                for part in (HI, LO):
                    mm = pe.matmul(bank[ZB[s % 3]][:, :], vw[:, part, RP + j * PART:RP + (j + 1) * PART],
                                   wT[:, b % 2, :], start=False, stop=part == LO)
                mm.then_inc(s_z, 1)

            def second_layer(s):
                b, j = divmod(s, NB)
                g = GROUP_OF[j]
                c = j - FIRST[g]
                pe.wait_ge(s_hlo, s + 1)
                if b == 0 and g == 0 and c == 0:
                    pe.wait_ge(s_gwhi, 1)
                    pe.wait_ge(s_gwlo, 1)
                if b == 0 and g > 0 and c % 2 == 0:
                    pe.wait_ge(s_flo, 2 * (g - 1) + c // 2 + 1)
                    pe.wait_ge(s_fhi, 2 * (g - 1) + c // 2 + 1)
                for half in range(2):
                    u = 2 * (NG * b + g) + half
                    if c == 0:
                        take(AB[u % 3], (s_comb, u + 1))
                    for t in (2 * half, 2 * half + 1):
                        o = bank[AB[u % 3]][:, (t % 2) * H:(t % 2 + 1) * H]
                        for i, (a, w) in enumerate(SPLIT_PASSES):
                            rhs = gw2[:, w, c, :] if g == 0 else w2[:, w, j - GB, :]
                            mm = pe.matmul(o, h[:, s % HRING, a, t * PART:(t + 1) * PART], rhs,
                                           start=c == 0 and i == 0 and t % 2 == 0,
                                           stop=c == COUNT[g] - 1 and i == 2 and t % 2 == 1,
                                           skip_group_check=True)
                    if half == 0 and c == COUNT[g] - 1:
                        mm.then_inc(s_acc, 1)
                if c == COUNT[g] - 1:
                    mm.then_inc(s_acc, 1)
                else:
                    mm.then_inc(s_w2, 1)

            first_layer_nx(0)
            b2_product()
            w_transpose(0)
            first_layer_nx(1)
            logits(0)
            for s in range(SLOTS + LAG):
                b, j = divmod(s, NB)
                if s < SLOTS:
                    if s == 0:
                        first_layer_evidence(s)
                    run_plan(steps, "pe", b, j, "pre")
                    if s >= EARLY:
                        first_layer_nx(s)
                    if s > 0:
                        first_layer_evidence(s)
                if s >= LAG:
                    second_layer(s - LAG)

        def h_free(eng, s):
            b, j = divmod(s, NB)
            g = GROUP_OF[j]
            if j == FIRST[g] + COUNT[g] - 1:
                eng.wait_ge(s_acc, 2 * (NG * b + g + 1))
            else:
                eng.wait_ge(s_w2, s + 1 - (NG * b + g))

        @blk.scalar
        def _(act):
            for name in small:
                load_rows(act, name)

            def nx_hi(b):
                for k in range(KC):
                    act.wait_ge(s_nf, KC * b + k + 1)
                    if b >= 2 and k == 0:
                        act.wait_ge(s_z, NB * (b - 1))
                    act.copy(nx[:, b % 2, HI, k, :], nxf[:, k, :]).then_inc(s_nhi, 1)

            def exp(b):
                act.wait_ge(s_sc, b + 1)
                if b >= 1:
                    act.wait_ge(s_wc, b)
                for half in range(2):
                    act.copy(sm_e[:, 2 * half:2 * half + 2, :], score_parts(half)[:, :, 1, :]).then_inc(s_cross, 1)
                act.wait_ge(s_d, b + 1)
                act.activation(sm_e[:, :, 0:NP], sm_d[:, :, 0:NP], ACT.Exp, scale=H ** -0.5).then_inc(s_e, 1)

            def wT_copy(b):
                act.wait_ge(s_wt, b + 1)
                if b >= 2:
                    act.wait_ge(s_z, NB * (b - 1))
                act.copy(wT[:, b % 2, :], bank[MB[1]][:, :]).then_inc(s_wT, 1)

            def exp_router(b):
                act.wait_ge(s_d3, b + 1)
                act.activation(lge[:, :, 0:E], lgd[:, :, 0:E], ACT.Exp).then_inc(s_e3, 1)

            def pair_hi(pair, g, src=None):
                act.wait_ge(s_vwp, NG * pair + g + 1)
                if pair >= 1:
                    act.wait_ge(s_dup[g], 32 * 2 * pair)
                src = bank[src if src is not None else PAIR_BANK[g]]
                act.copy(vw_pair[:, HI, VCOLS[g]], src[:, 0:VCOLS[g].stop - VCOLS[g].start]).then_inc(s_phi, 1)

            def ew_copy(e):
                act.wait_ge(s_ewT, e + 1)
                if e >= 1:
                    act.wait_ge(s_fold, 2 * e)
                else:
                    act.wait_ge(s_b2p, 1)
                for k in range(KC):
                    act.copy(ewT[:, k, :], bank[MB[k]][:, :]).then_inc(s_ewc, 1)

            def fold_hi(e):
                for i in range(2):
                    act.wait_ge(s_fold, 2 * e + i + 1)
                    act.copy(w2[:, HI, e * EB + 2 * i:e * EB + 2 * i + 2, :].rearrange("p i h -> p (i h)"),
                             bank[MB[i]][:, :]).then_inc(s_fhi, 1)

            def gate_tanh(b):
                act.wait_ge(s_comb, 2 * (NG * b + 1))
                act.activation(tg, tg, ACT.Tanh, scale=0.5).then_inc(s_tg, 1)

            def w1_hi(g):
                i, arrived = stage_of("n", g)
                act.wait_ge(*arrived)
                act.copy(w1n[:, HI, :, COLS[g]], stage[:, i, :, 0:COUNT[g] * PART]).then_inc(s_w1hi, 1)

            def v_hi(n):
                if n == NG:
                    act.copy(vT_hi, vT[:, :, PART:]).then_inc(s_vhi, 1)
                    return
                if n == 0:
                    act.wait_ge(s_fold, 2 * E)
                else:
                    last = [p for i, p in enumerate(staged) if i % STAGES == HI_STAGE[n]][-1]
                    act.wait_ge(*{("n", NG - 1): (s_w1lo, NG), ("c", NG - 1): (s_zbc, NG),
                                  ("w2", E - 1): (s_ewT, E)}[last])
                act.copy(w1v_hi[n], w1v[:, :, VCOLS[n]]).then_inc(s_vhi, 1)

            steps = {"v_hi": v_hi, "nx_hi": nx_hi, "exp": exp, "wT_copy": wT_copy, "exp_router": exp_router,
                     "pair_hi": pair_hi, "ew_copy": ew_copy, "fold_hi": fold_hi, "gate_tanh": gate_tanh,
                     "w1_hi": w1_hi}

            def prep(name, dst, i):
                act.wait_ge(s_prep, PREP[name])
                act.copy(dst, bank[i][:, :]).then_inc(s_pa, 1)

            prep("pT1", pT[:, 1, :], 3)
            prep("vT0", vT[:, 0, :], 2)
            prep("vT1", vT[:, 1, :], 3)
            nx_hi(0)
            w1_hi(0)
            for i in range(KC):
                act.wait_ge(s_prep, PREP[f"qk{i}"])
                act.copy(qkr[:, HI, i, :, 0:NP], bank[i][:, :].rearrange("p (b n) -> p b n", b=B)).then_inc(s_pa, 1)
            pair_hi(0, 0, src=FIRST_PAIR_BANK[0])
            pair_hi(0, 1, src=FIRST_PAIR_BANK[1])
            exp(0)
            w1_hi(1)
            wT_copy(0)
            act.wait_ge(s_gw2, 16)
            act.copy(gw2[:, HI, :, :], gw2_raw).then_inc(s_gwhi, 1)
            exp_router(0)

            for s in range(SLOTS):
                b, j = divmod(s, NB)
                run_plan(steps, "act", b, j, "pre")
                if b == 0 and j == FIRST[GROUP_OF[j]]:
                    act.wait_ge(s_zb, GROUP_OF[j] + 1)
                if s == 1:
                    act.wait_ge(s_gwlo, 1)
                act.wait_ge(s_z, s + 1)
                if s >= 2:
                    act.wait_ge(s_hlo, s - 1)
                z = bank[ZB[s % 3]][:, :]
                act.activation(hf[:, s % 2, :], z, ACT.Silu, bias=zb[:, j, b:b + 1]).then_inc(s_h, 1)
                if s >= HRING:
                    h_free(act, s - HRING)
                act.activation(h[:, s % HRING, HI, :], z, ACT.Silu, bias=zb[:, j, b:b + 1]).then_inc(s_h, 1)
                run_plan(steps, "act", b, j, "post")

        @blk.vector
        def _(dve):
            chain = 0

            def link(ins):
                nonlocal chain
                chain += 1
                ins.then_inc(s_vc, 1)
                dve.wait_ge(s_vc, chain)

            def stats_of(b):
                dve.wait_ge(s_x[b % XBUFS], 16 * (b // XBUFS + 1))
                for t in range(NT):
                    ins = dve.bn_stats(stats[:, t, :], xbuf[:, b % XBUFS, t, :])
                link(ins)
                for t in range(NT):
                    ins = dve.bn_aggr(mv[:, t, :], stats[:, t, :])
                link(ins)
                if b >= 1:
                    dve.wait_ge(s_rstd, b)
                dve.tensor_scalar(ve[:, :], mv[:, :, 1], LN_EPS, None, ALU.add).then_inc(s_ve, 1)

            def normalise(b):
                dve.wait_ge(s_rstd, b + 1)
                if b >= 1:
                    dve.wait_ge(s_nhi, KC * b)
                    dve.wait_ge(s_nlo, KC * b)
                for t in range(NT):
                    ins = dve.tensor_scalar(xhat[:, t, :], xbuf[:, b % XBUFS, t, :], mv[:, t, 0:1],
                                            rstd[:, t:t + 1], ALU.subtract, ALU.mult)
                ins.then_inc(s_xhat, 1)

            def nx_full(b):
                dve.wait_ge(s_xT, b + 1)
                for k in range(KC):
                    dve.tensor_scalar(nxf[:, k, :], bank[MB[k]][:, :], cols[:, C_GAMMA + k:C_GAMMA + k + 1],
                                      cols[:, C_BETA + k:C_BETA + k + 1], ALU.mult, ALU.add).then_inc(s_nf, 1)

            def nx_lo(b):
                if b >= 2:
                    dve.wait_ge(s_z, NB * (b - 1))
                for k in range(KC):
                    dve.wait_ge(s_nhi, KC * b + k + 1)
                    dve.tensor_tensor(nx[:, b % 2, LO, k, :], nxf[:, k, :],
                                      nx[:, b % 2, HI, k, :].bitcast(F32), ALU.subtract).then_inc(s_nlo, 1)

            def over_last(v, n):
                return v.unsqueeze(2).broadcast_to([PART, NT, n])

            def score_max(b):
                dve.wait_ge(s_sc, b + 1)
                if b >= 1:
                    dve.wait_ge(s_wc, b)
                for half in range(2):
                    dve.wait_ge(s_cross, 2 * b + half + 1)
                    tiles = slice(2 * half, 2 * half + 2)
                    dve.tensor_tensor(sm_d[:, tiles, :], score_parts(half)[:, :, 0, :], sm_e[:, tiles, :],
                                      ALU.add).then_inc(s_s, 1)
                dve.wait_ge(s_s, 2 * b + 2)
                s = sm_d[:, :, 0:NP]
                dve.tensor_reduce(red[:, 0, :], s, AX_X, ALU.max).then_inc(s_max, 1)
                bias = lb_bc[:, b, :].unsqueeze(1).broadcast_to([PART, NT, RP])
                if b >= 1:
                    dve.wait_ge(s_lgin, b)
                dve.tensor_tensor(lgn[:, :, :], sm_d[:, :, NP:SC], bias, ALU.add).then_inc(s_lgn, 1)
                dve.wait_ge(s_max, b + 1)
                dve.tensor_tensor(s, s, over_last(red[:, 0, :], NP), ALU.subtract).then_inc(s_d, 1)

            def weights(b):
                dve.wait_ge(s_e, b + 1)
                link(dve.tensor_reduce(red[:, 1, :], sm_e[:, :, 0:NP], AX_X, ALU.add))
                link(dve.reciprocal(red[:, 2, :], red[:, 1, :]))
                link(dve.tensor_tensor(sm_d[:, :, 0:NP], sm_e[:, :, 0:NP], over_last(red[:, 2, :], NP), ALU.mult))
                if b >= 1:
                    dve.wait_ge(s_wt, b)
                link(dve.tensor_copy(wcat[:, :, HI, :], sm_d[:, :, 0:NP]))
                dve.tensor_tensor(wcat[:, :, LO, :], sm_d[:, :, 0:NP], wcat[:, :, HI, :].bitcast(F32),
                                  ALU.subtract).then_inc(s_wc, 1)

            def router_max(b):
                dve.wait_ge(s_lg, b + 1)
                dve.wait_ge(s_lgn, b + 1)
                src = bank[MB[1]][:, 0:NT * 2 * RP].rearrange("p (t a c) -> p t a c", t=NT, a=2)
                link(dve.tensor_tensor(lgn[:, :, :], src[:, :, LO, :], lgn[:, :, :], ALU.add))
                dve.tensor_tensor(lg[:, :, :], src[:, :, HI, :], lgn[:, :, :], ALU.add).then_inc(s_lgin, 1)
                dve.wait_ge(s_lgin, b + 1)
                link(dve.tensor_reduce(red3[:, 0, :], lg[:, :, 0:E], AX_X, ALU.max))
                if b >= 1:
                    dve.wait_ge(s_e3, b)
                dve.tensor_tensor(lgd[:, :, 0:E], lg[:, :, 0:E], over_last(red3[:, 0, :], E),
                                  ALU.subtract).then_inc(s_d3, 1)

            def router_prob(b):
                dve.wait_ge(s_e3, b + 1)
                link(dve.tensor_reduce(red3[:, 1, :], lge[:, :, 0:E], AX_X, ALU.add))
                link(dve.reciprocal(red3[:, 2, :], red3[:, 1, :]))
                link(dve.tensor_scalar(red3[:, 3, :], red3[:, 2, :], 0.5, None, ALU.mult))
                if b >= 2:
                    dve.wait_ge(s_bs, b - 1)
                dve.tensor_tensor(ph[:, b % 2, :, 0:E], lge[:, :, 0:E], over_last(red3[:, 3, :], E),
                                  ALU.mult).then_inc(s_ph, 1)

            def pair_lo(pair, g, src=None):
                dve.wait_ge(s_phi, NG * pair + g + 1)
                src = bank[src if src is not None else PAIR_BANK[g]]
                dve.tensor_tensor(vw_pair[:, LO, VCOLS[g]], src[:, 0:VCOLS[g].stop - VCOLS[g].start],
                                  vw_pair[:, HI, VCOLS[g]].bitcast(F32), ALU.subtract).then_inc(s_plo, 1)

            def fold_lo(e):
                for i in range(2):
                    dve.wait_ge(s_fhi, 2 * e + i + 1)
                    blocks = slice(e * EB + 2 * i, e * EB + 2 * i + 2)
                    dve.tensor_tensor(w2[:, LO, blocks, :].rearrange("p i h -> p (i h)"), bank[MB[i]][:, :],
                                      w2[:, HI, blocks, :].rearrange("p i h -> p (i h)").bitcast(F32),
                                      ALU.subtract).then_inc(s_flo, 1)

            def w1_lo(g):
                i, _ = stage_of("n", g)
                dve.wait_ge(s_w1hi, g + 1)
                dve.tensor_tensor(w1n[:, LO, :, COLS[g]], stage[:, i, :, 0:COUNT[g] * PART],
                                  w1n[:, HI, :, COLS[g]].bitcast(F32), ALU.subtract).then_inc(s_w1lo, 1)

            def z_bias(g):
                blocks = slice(FIRST[g], FIRST[g] + COUNT[g])
                dve.wait_ge(s_zbc, g + 1)
                dve.tensor_tensor(zb[:, blocks, :],
                                  bank[ZBIAS_BANK[g]][:, 0:COUNT[g] * B].rearrange("p (j b) -> p j b", b=B),
                                  cols[:, C_B1 + FIRST[g]:C_B1 + FIRST[g] + COUNT[g]].unsqueeze(2)
                                  .broadcast_to([PART, COUNT[g], B]), ALU.add).then_inc(s_zb, 1)

            def b2_out():
                dve.wait_ge(s_bc, 32)
                dve.wait_ge(s_b2p, 1)
                dve.tensor_tensor(b2o[:, 0:2, :], bank[B2_BANK[0]][:, :].rearrange("p (e h) -> p e h", e=2),
                                  outb_bc[:, :].unsqueeze(1).broadcast_to([PART, 2, H]), ALU.add).then_inc(s_b2o, 1)
                dve.tensor_tensor(b2o[:, 2, :], bank[B2_BANK[1]][:, 0:H], outb_bc[:, :], ALU.add).then_inc(s_b2o, 1)

            def v_lo(n):
                name = "vT" if n == NG else f"w1v{n}"
                dve.wait_ge(s_vhi, VSPLIT[name])
                if n == NG:
                    src, lo, hi = vT[:, :, PART:], vT_lo[:, :, PART:], vT_hi
                else:
                    dve.wait_ge(s_vwp, n + 1)
                    src, lo, hi = w1v[:, :, VCOLS[n]], w1v_lo[:, :, VCOLS[n]], w1v_hi[n]
                dve.tensor_tensor(lo, src, hi.bitcast(F32), ALU.subtract).then_inc(s_vlo, 1)

            steps = {"v_lo": v_lo, "stats": stats_of, "normalise": normalise, "nx_full": nx_full, "nx_lo": nx_lo,
                     "score_max": score_max, "weights": weights, "router_max": router_max,
                     "router_prob": router_prob, "pair_lo": pair_lo, "fold_lo": fold_lo, "w1_lo": w1_lo,
                     "z_bias": z_bias}

            done = 0

            def prep(name, ins):
                nonlocal done
                done += 1
                assert PV[name] == done
                ins.then_inc(s_pv, 1)

            def prep_copy(name, dst, i, n=512):
                dve.wait_ge(s_prep, PREP[name])
                prep(name, dve.tensor_copy(dst, bank[i][:, 0:n]))

            dve.memset(ones8[:, :], 1.0)
            prep_copy("wkT", wkT.rearrange("p k n -> p (k n)"), 0)
            prep_copy("wqT", wqT.rearrange("p k n -> p (k n)"), 1)
            prep_copy("pT0", pT[:, 0, :], 2)
            stats_of(0)
            prep_copy("gT", gT.rearrange("p k n -> p (k n)"), 4)
            normalise(0)
            prep_copy("cols", cols[:, :], 5, NROWS)
            dve.wait_ge(s_pv, PV["cols"])
            nx_full(0)
            nx_lo(0)
            dve.wait_ge(s_wr, 32)
            dve.wait_ge(s_prep, PREP["lb"])
            link(dve.memset(lb[:, :], 0.0))
            link(dve.tensor_tensor(lb[:, 0:E], bank[5][0:8, 0:E], rb_bc[:, :], ALU.add))
            dve.wait_ge(s_pool0, 2)
            prep("lb", dve.tensor_tensor(lb_diag[:, :, :], ident[0:8, 0:B].unsqueeze(2).broadcast_to([8, B, RP]),
                                         lb[:, :].unsqueeze(1).broadcast_to([8, B, RP]), ALU.mult))
            for i in range(KC):
                dve.wait_ge(s_pa, PA[f"qk{i}"])
                src = bank[i][:, :].rearrange("p (b n) -> p b n", b=B)
                prep(f"qk{i}", dve.tensor_tensor(qkr[:, LO, i, :, 0:NP], src, qkr[:, HI, i, :, 0:NP].bitcast(F32),
                                                 ALU.subtract))
            prep_copy("lb_bc", lb_bc[:, :, :].rearrange("p b c -> p (b c)"), 5, B * RP)
            w1_lo(0)
            pair_lo(0, 0, src=FIRST_PAIR_BANK[0])
            dve.wait_ge(s_pv, PV["lb_bc"])
            score_max(0)
            pair_lo(0, 1, src=FIRST_PAIR_BANK[1])
            weights(0)
            z_bias(0)
            w1_lo(1)
            b2_out()
            router_max(0)
            dve.wait_ge(s_gwhi, 1)
            dve.tensor_tensor(gw2[:, LO, :, :], gw2_raw, gw2[:, HI, :, :].bitcast(F32), ALU.subtract)\
               .then_inc(s_gwlo, 1)
            router_prob(0)

            def combine(b, g, half):
                u = 2 * (NG * b + g) + half
                tiles = slice(2 * half, 2 * half + 2)
                dve.wait_ge(s_acc, u + 1)
                src = bank[AB[u % 3]][:, :].rearrange("p (i h) -> p i h", i=2)
                if g == 0:
                    if b >= 1:
                        dve.wait_ge(s_y, 2 * b)
                    dve.tensor_tensor(tg[:, tiles, :], src, gb2_bc[:, :].unsqueeze(1)
                                      .broadcast_to([PART, 2, H]), ALU.add).then_inc(s_comb, 1)
                    return
                if g == 1 and half == 0:
                    dve.wait_ge(s_bs, b + 1)
                    if b >= 1:
                        dve.wait_ge(s_o, 2 * b)
                if g > 1:
                    dve.wait_ge(s_comb, u - 1)
                for i in range(2):
                    t = 2 * half + i
                    ins = dve.scalar_tensor_tensor(acc[:, t, :], src[:, i, :], ph[:, b % 2, t, g - 1:g],
                                                   (bsum if g == 1 else acc)[:, t, :], ALU.mult, ALU.add)
                ins.then_inc(s_comb, 1)

            def gated(b, half):
                tiles = slice(2 * half, 2 * half + 2)
                dve.wait_ge(s_tg, b + 1)
                dve.wait_ge(s_comb, 2 * NG * (b + 1) - 1 + half)
                dve.scalar_tensor_tensor(acc[:, tiles, :], tg[:, tiles, :], 1.0, acc[:, tiles, :],
                                         ALU.add, ALU.mult).then_inc(s_y, 1)

            def all_but_last(half):
                b = B - 1
                tiles = slice(2 * half, 2 * half + 2)
                dve.wait_ge(s_tg, b + 1)
                dve.wait_ge(s_comb, 2 * (NG * b + NG - 1) - 1 + half)
                link(dve.scalar_tensor_tensor(acc[:, tiles, :], tg[:, tiles, :], 1.0, acc[:, tiles, :],
                                              ALU.add, ALU.mult))
                xt = xbuf[:, b % XBUFS, tiles, :]
                dve.tensor_tensor(xt, xt, acc[:, tiles, :], ALU.add)
                link(dve.scalar_tensor_tensor(bsum[:, tiles, :], tg[:, tiles, :], 1.0,
                                              ph[:, b % 2, tiles, E - 1:E].broadcast_to([PART, 2, H]),
                                              ALU.add, ALU.mult))

            def last_expert(half):
                b = B - 1
                u = 2 * (NG * b + NG - 1) + half
                tiles = slice(2 * half, 2 * half + 2)
                dve.wait_ge(s_acc, u + 1)
                src = bank[AB[u % 3]][:, :].rearrange("p (i h) -> p i h", i=2)
                link(dve.tensor_tensor(acc[:, tiles, :], src, bsum[:, tiles, :], ALU.mult))
                xt = xbuf[:, b % XBUFS, tiles, :]
                dve.tensor_tensor(xt, xt, acc[:, tiles, :], ALU.add).then_inc(s_o, 1)

            for s in range(SLOTS + LAG):
                b, j = divmod(s, NB)
                if s < SLOTS:
                    run_plan(steps, "dve", b, j, "pre")
                    dve.wait_ge(s_h, 2 * (s + 1))
                    if s >= HRING:
                        h_free(dve, s - HRING)
                    dve.tensor_tensor(h[:, s % HRING, LO, :], hf[:, s % 2, :],
                                      h[:, s % HRING, HI, :].bitcast(F32), ALU.subtract).then_inc(s_hlo, 1)
                if s >= LAG:
                    b2, j2 = divmod(s - LAG, NB)
                    g = GROUP_OF[j2]
                    if j2 == FIRST[g] + COUNT[g] - 1:
                        for half in range(2):
                            if b2 == B - 1 and g == NG - 1:
                                last_expert(half)
                                continue
                            combine(b2, g, half)
                            if g == NG - 1:
                                gated(b2, half)
                if SLOTS - 2 <= s < SLOTS:
                    all_but_last(s - (SLOTS - 2))
                if s < SLOTS:
                    run_plan(steps, "dve", b, j, "post")

        @blk.gpsimd
        def _(pool):
            chain = 0

            def link(ins):
                nonlocal chain
                chain += 1
                ins.then_inc(s_gc, 1)
                pool.wait_ge(s_gc, chain)

            def reciprocal_std(b):
                pool.wait_ge(s_ve, b + 1)
                if b >= 1:
                    pool.wait_ge(s_xhat, b)
                pool.tensor_tensor(rstd[:, :], ve[:, :], minus_half[:, :], ALU.pow).then_inc(s_rstd, 1)

            def bias_sum(b):
                pool.wait_ge(s_ph, b + 1)
                pool.wait_ge(s_b2o, 2)
                if b >= 1:
                    pool.wait_ge(s_comb, 2 * (NG * (b - 1) + 2))
                for t in range(NT):
                    p = ph[:, b % 2, t, :]
                    pool.tensor_scalar(bsum[:, t, :], b2o[:, 0, :], p[:, 0:1], 0.0, ALU.mult, ALU.add)
                    for e in (1, 2):
                        ins = pool.tensor_scalar(btmp[:, e - 1, :], b2o[:, e, :], p[:, e:e + 1], 0.0,
                                                 ALU.mult, ALU.add)
                    link(ins)
                    link(pool.tensor_tensor(bsum[:, t, :], bsum[:, t, :], btmp[:, 0, :], ALU.add))
                    ins = pool.tensor_tensor(bsum[:, t, :], bsum[:, t, :], btmp[:, 1, :], ALU.add)
                    if t < NT - 1:
                        link(ins)
                ins.then_inc(s_bs, 1)

            pool.memset(minus_half[:, :], -0.5)
            pool.memset(ident[:, :], 0.0).then_inc(s_pool0, 1)
            pool.wait_ge(s_pool0, 1)
            pool.affine_select(out=ident[:, :], in_=ident[:, :], compare_op=ALU.not_equal, fill=1.0, base=0,
                               pattern=[[-1, PART]], channel_multiplier=1).then_inc(s_pool0, 1)
            pool.memset(wr[:, :, :], 0.0).then_inc(s_pool0, 1)
            pool.wait_ge(s_pool0, 3)
            pool.dma_start(wr[:, :, 0:E], router_W.rearrange("(k p) e -> p k e", p=PART)).then_inc(s_wr, 16)
            pool.dma_start(rb_bc[:, :], router_b.partition_broadcast(8)).then_inc(s_wr, 16)
            pool.dma_start(gw2_raw, gate_w2.rearrange("(k p) n -> p k n", p=PART)).then_inc(s_gw2, 16)
            pool.dma_start(outb_bc[:, :], out_b.partition_broadcast(PART)).then_inc(s_bc, 16)
            pool.dma_start(gb2_bc[:, :], gate_b2.partition_broadcast(PART)).then_inc(s_bc, 16)
            pool.tensor_copy(ident_r[:, :], ident[:, :]).then_inc(s_pool0, 1)
            pool.wait_ge(s_wr, 32)
            pool.tensor_copy(w1v[:, :, 0:RP], wr[:, KC:2 * KC, :]).then_inc(s_pool0, 1)
            wr_nx = wr[:, 0:KC, :].unsqueeze(2).broadcast_to([PART, KC, B, RP])
            pool.tensor_copy(qkr[:, HI, :, :, NP:SC], wr_nx).then_inc(s_pool0, 1)
            pool.wait_ge(s_pool0, 6)
            pool.tensor_tensor(qkr[:, LO, :, :, NP:SC], wr_nx, qkr[:, HI, :, :, NP:SC].bitcast(F32),
                               ALU.subtract).then_inc(s_pool0, 1)
            reciprocal_std(0)
            pool.wait_ge(s_pv, PV["cols"])
            pool.wait_ge(s_prep, PREP["gT"])
            pool.tensor_copy(b2_bc, cols[:, C_B2:C_B2 + E * KC].unsqueeze(2)
                             .broadcast_to([PART, E * KC, PART])).then_inc(s_pool0, 1)
            reciprocal_std(1)
            bias_sum(0)
            for b in range(B):
                for half in range(2 if b >= 1 else 0):
                    pool.wait_ge(s_y, 2 * (b - 1) + half + 1)
                    tiles = slice(2 * half, 2 * half + 2)
                    xt = xbuf[:, (b - 1) % XBUFS, tiles, :]
                    pool.tensor_tensor(xt, xt, acc[:, tiles, :], ALU.add).then_inc(s_o, 1)
                if b + 2 < B:
                    reciprocal_std(b + 2)
                if b + 1 < B:
                    bias_sum(b + 1)


_INS = ["x", "cond_1024", "ctx_1024", "L0_xcond_ln_gamma", "L0_xcond_ln_beta", "L0_xcond_Wq", "L0_xcond_Wk",
        "L0_xcond_Wv", "L0_xcond_router_W", "L0_xcond_router_b", "L0_xcond_e_w1", "L0_xcond_e_b1",
        "L0_xcond_e_w2", "L0_xcond_e_b2", "L0_xcond_gate_w1", "L0_xcond_gate_b1", "L0_xcond_gate_w2",
        "L0_xcond_gate_b2", "L0_xcond_out_w", "L0_xcond_out_b"]


def kernel(**inputs):
    import numpy as _np
    import concourse.bacc as _bacc
    from concourse import mybir as _mybir
    from concourse.bass_utils import run_bass_kernel_spmd as _run

    nc = _bacc.Bacc("TRN2", target_bir_lowering=False, num_devices=1)
    arrays, args = {}, []
    for name in _INS:
        a = _np.ascontiguousarray(inputs[name])
        arrays[f"in_{name}_dram"] = a
        args.append(nc.dram_tensor(f"in_{name}_dram", a.shape, _mybir.dt.from_np(a.dtype), kind="ExternalInput").ap())
    shape = tuple(inputs["x"].shape)
    args.append(nc.dram_tensor("out_0_dram", shape, _mybir.dt.float32, kind="ExternalOutput").ap())
    build(nc, *args)
    r = _run(nc, [arrays], core_ids=[0])
    return r.results[0]["out_0_dram"]
```
